# Optimizing a Trainium2 kernel written in Bass

```python
import numpy as np
import jax
import jax.numpy as jnp

def _softmax(x, axis=-1):
    return jax.nn.softmax(x, axis=axis)
def _gelu(x):
    return jax.nn.gelu(x, approximate=True)
def _silu(x):
    return jax.nn.silu(x)
def _sigmoid(x):
    return jax.nn.sigmoid(x)
def _layernorm(x, axis=-1, eps=1e-5):
    m = jnp.mean(x, axis=axis, keepdims=True)
    v = jnp.var(x, axis=axis, keepdims=True)
    return (x - m) / jnp.sqrt(v + eps)
def _scatter_add(tgt, idx, src, axis=0):
    return tgt.at[idx].add(src)
def _segment_sum(src, seg, n):
    return jax.ops.segment_sum(src, seg, n)

kernel_name = 'mk_conv_preact_d2_conv_nchw512_6dc32e'

def setup_inputs(seed: int = 0):
    np.random.seed(seed)
    _w = jnp.asarray
    def _rec_inputs():
        import jax
        import jax.numpy as jnp
        _gk = jax.random.key(seed)
        x = -9.26e-05 + 0.9999 * jax.random.normal(jax.random.fold_in(_gk, 1), (32, 512, 48, 48), jnp.float32)
        return x
    x = _rec_inputs()
    def _L0_conv_setup():
        import jax, jax.numpy as jnp
        import numpy as np
        K = 3
        M = 4
        key = jax.random.key(seed)
        ks = jax.random.split(key, 10)
        N, C, H, W = (32, 512, 48, 48)
        Cm = C // M
        P = 512
        sc = 0.05
        x = jax.random.normal(ks[0], (N, C, H, W), jnp.float32)
        Wc = jax.random.normal(ks[1], (Cm, C), jnp.float32) * sc
        bc = jax.random.normal(ks[2], (Cm,), jnp.float32) * sc
        Wkk = jax.random.normal(ks[3], (K * K,), jnp.float32) * sc
        bkk = jax.random.normal(ks[4], (K * K,), jnp.float32) * sc
        Wck = jax.random.normal(ks[5], (Cm, 2), jnp.float32) * sc
        bck = jax.random.normal(ks[6], (Cm,), jnp.float32) * sc
        b_ad = jax.random.normal(ks[7], (Cm,), jnp.float32) * sc
        Wf = jax.random.normal(ks[8], (P, Cm), jnp.float32) * sc
        bf = jax.random.normal(ks[9], (P,), jnp.float32) * sc
        return {'x': x, 'Wc': Wc, 'bc': bc, 'Wkk': Wkk, 'bkk': bkk, 'Wck': Wck, 'bck': bck, 'b_ad': b_ad, 'Wf': Wf, 'bf': bf}
    _L0_conv_all = _L0_conv_setup()
    _L0_conv_in = {k: v for k, v in _L0_conv_all.items() if k in ('Wc', 'bc', 'Wkk', 'bkk', 'Wck', 'bck', 'b_ad', 'Wf', 'bf', )}
    del _L0_conv_all

    def _L1_conv_setup():
        import jax, jax.numpy as jnp
        import numpy as np
        key = jax.random.key(seed)
        k1, k2 = jax.random.split(key)
        B, Cin, Cout, K, H, W = (32, 16, 16, 3, 256, 256)
        x = jax.random.normal(k1, (1, B * Cin, H, W), dtype=jnp.float32)
        kernels = jax.random.normal(k2, (B * Cout, Cin, K, K), dtype=jnp.float32)
        return {'x': x, 'kernels': kernels, 'batch_size': B}
    _L1_conv_all = _L1_conv_setup()
    _L1_conv_in = {k: v for k, v in _L1_conv_all.items() if k in ('kernels', )}
    del _L1_conv_all

    return {
        "x": x,
        "L0_conv_Wc": _L0_conv_in["Wc"],
        "L0_conv_bc": _L0_conv_in["bc"],
        "L0_conv_Wkk": _L0_conv_in["Wkk"],
        "L0_conv_bkk": _L0_conv_in["bkk"],
        "L0_conv_Wck": _L0_conv_in["Wck"],
        "L0_conv_bck": _L0_conv_in["bck"],
        "L0_conv_b_ad": _L0_conv_in["b_ad"],
        "L0_conv_Wf": _L0_conv_in["Wf"],
        "L0_conv_bf": _L0_conv_in["bf"],
        "L1_conv_kernels": _L1_conv_in["kernels"],
    }

def reference(x, L0_conv_Wc, L0_conv_bc, L0_conv_Wkk, L0_conv_bkk, L0_conv_Wck, L0_conv_bck, L0_conv_b_ad, L0_conv_Wf, L0_conv_bf, L1_conv_kernels):
    import jax
    import jax.numpy as jnp
    def _L0_conv_ref(x, Wc, bc, Wkk, bkk, Wck, bck, b_ad, Wf, bf):
        import jax, jax.numpy as jnp
        import numpy as np
        K = 3
        M = 4
        N, C, H, W = x.shape
        Cm = Wc.shape[0]
        k = K
        pad = (k - 1) // 2
        f = jax.nn.relu(jnp.einsum('oc,nchw->nohw', Wc, x) + bc[None, :, None, None])
        gk1 = jax.nn.relu(jnp.mean(x, axis=(2, 3)) @ Wc.T + bc)
        g_kern = (gk1[:, :, None] * Wkk[None, None, :] + bkk[None, None, :]).reshape(N, Cm, k, k)
        xm = x.reshape(N, C, k, H // k, k, W // k).max(axis=(3, 5))
        sk = jax.nn.relu(jnp.einsum('oc,nckl->nokl', Wc, xm) + bc[None, :, None, None])
        gs = jnp.stack([g_kern, sk], axis=2)
        dynW = jax.nn.relu(jnp.einsum('oj,ncjkl->nockl', Wck, gs) + bck[None, :, None, None, None])

        def conv_one(fn, wn):
            return jax.lax.conv_general_dilated(fn[None], wn, window_strides=(1, 1), padding=[(pad, pad), (pad, pad)])[0]
        y = jax.vmap(conv_one)(f, dynW) + b_ad[None, :, None, None]
        out = jnp.einsum('oc,nchw->nohw', Wf, y) + bf[None, :, None, None]
        return out

    def _L1_conv_ref(x, kernels, batch_size):
        import jax, jax.numpy as jnp
        import numpy as np
        return jax.lax.conv_general_dilated(x, kernels, window_strides=(1, 1), padding='SAME', dimension_numbers=('NCHW', 'OIHW', 'NCHW'), feature_group_count=batch_size)

    def _gn(v, G=32, eps=1e-5):
        B_, C_, H_, W_ = v.shape
        g = v.reshape(B_, G, C_ // G, H_, W_)
        m = jnp.mean(g, axis=(2, 3, 4), keepdims=True)
        s = jnp.var(g, axis=(2, 3, 4), keepdims=True)
        return ((g - m) / jnp.sqrt(s + eps)).reshape(v.shape)

    def _ln_c(v, eps=1e-6):
        m = jnp.mean(v, axis=1, keepdims=True)
        s = jnp.var(v, axis=1, keepdims=True)
        return (v - m) / jnp.sqrt(s + eps)

    def _ln_t(v, eps=1e-5):
        m = jnp.mean(v, axis=-1, keepdims=True)
        s = jnp.var(v, axis=-1, keepdims=True)
        return (v - m) / jnp.sqrt(s + eps)

    def _to_tokens(v):
        B_, C_, H_, W_ = v.shape
        return v.reshape(B_, C_, H_ * W_).transpose(0, 2, 1)
    def _from_tokens(t, like):
        B_, C_, H_, W_ = like.shape
        return t.transpose(0, 2, 1).reshape(B_, C_, H_, W_)

    x = x + _L0_conv_ref(_gn(x), L0_conv_Wc, L0_conv_bc, L0_conv_Wkk, L0_conv_bkk, L0_conv_Wck, L0_conv_bck, L0_conv_b_ad, L0_conv_Wf, L0_conv_bf)
    x = x + _L1_conv_ref(_gn(x), L1_conv_kernels, 32)
    return x


_drawn_inputs = setup_inputs


def setup_inputs(seed=0):
    import zlib

    import numpy as np

    out = dict(_drawn_inputs(seed))
    spreads = {}
    factors = {'L0_conv_bc': 8.0,
     'L0_conv_Wkk': 64.0,
     'L0_conv_bkk': 27.782,
     'L0_conv_b_ad': 44.279,
     'L0_conv_bf': 24.515}
    for name, (base, spread) in spreads.items():
        noise = np.random.default_rng([zlib.crc32(name.encode()), seed]).standard_normal(out[name].shape)
        drawn = base * np.exp(spread * noise) if base else spread * noise
        out[name] = jnp.asarray(drawn.astype(out[name].dtype))
    for name, factor in factors.items():
        out[name] = (out[name] * factor).astype(out[name].dtype)
    return out
```

```python
from contextlib import ExitStack

import concourse.bass as bass
from concourse import mybir

F32 = mybir.dt.float32
F32R = mybir.dt.float32r
F16 = mybir.dt.float16
ALU = mybir.AluOpType
ACT = mybir.ActivationFunctionType
AX = mybir.AxisListType

P = 128
N, C, H, W = 32, 512, 48, 48
Q = C // P
PX = H * W
CM = 128
TAPS = 9
GC = 16
GQ = P // GC
G = C // GC
OR_ = 6
IR = OR_ + 2
NB = H // OR_
M6 = OR_ * GC
BW = NB * W
SLOTS = H + 2
TILES = [(0, 10), (10, 10), (20, 10), (30, 10), (40, 8)]
NT = len(TILES)
MAXW = 480
UNITS = NT * Q
EPS = 1e-5
XSCALE = 256.0
WSCALE = 8192.0

XS_RING, HL_RING, U_RING = 3, 4, 2
C_BANKS = 3
EARLY = 3
PX_BLOCK = 16


def row_parts(r0, rows):
    out, r = [], r0
    while r < r0 + rows:
        e = min(r0 + rows, (r // OR_ + 1) * OR_)
        out.append((r, e - r))
        r = e
    return out


PARTS = [row_parts(r0, rows) for r0, rows in TILES]
PART_SUM = [sum(len(p) for p in PARTS[:t]) for t in range(NT + 1)]
X1_OPS = Q * PART_SUM[NT]


def x1_count(t, c):
    return Q * PART_SUM[t] + (c + 1) * len(PARTS[t])


def partition_of(p):
    return GC * {0: 6, 7: 7}.get(p, p - 1)


T_SLOT = [0, 1, 2, 0]


def build(nc, x, wct, bc, wkk, bkk, wck, bck, b_ad, wft, bf, kt, out):
    x_d = x.rearrange("n (q p) h w -> n p q (h w)", q=Q)
    scratch = nc.dram_tensor("x1_rows", (N, C, SLOTS, W), F32, kind="Internal").ap()
    sc_w = scratch.rearrange("n (q p) s w -> n p q (s w)", q=Q)
    sc_r = scratch.rearrange("n (q j c) s w -> n q c j (s w)", q=Q, c=GC)

    with ExitStack() as ctx:
        def sb(name, shape, dt=F32):
            return ctx.enter_context(nc.sbuf_tensor(name, shape, dt))

        def bank(name):
            return ctx.enter_context(nc.psum_tensor(name, [P, 512], F32))

        def sem(name):
            return ctx.enter_context(nc.semaphore(name))

        xb = sb("xb", [P, Q, PX])
        x1b = sb("x1b", [P, Q, OR_, NB, W])
        mrow = sb("mrow", [P, Q, W])
        tb = sb("tb", [P, 3, GQ, NB, W])
        fh = sb("fh", [P, H + 2, W + 2], F32R)
        fl = sb("fl", [P, H + 2, W + 2], F32R)
        k_h = sb("k_h", [P, G, 3, M6], F16)
        k_l = sb("k_l", [P, G, 3, M6], F16)
        xs = sb("xs", [P, XS_RING, 2, MAXW], F32R)
        yp = sb("yp", [P, 2, 2, MAXW], F32R)
        hl = sb("hl", [P, HL_RING, 2, NB, W + 2], F16)
        un = sb("un", [P, U_RING, NB, W])
        dynh = sb("dynh", [P, TAPS, CM], F32R)
        dynl = sb("dynl", [P, TAPS, CM], F32R)
        dtmp = sb("dtmp", [P, TAPS, CM])
        wc = sb("wc", [P, Q, CM])
        wch = sb("wch", [P, Q, CM], F32R)
        wcl = sb("wcl", [P, Q, CM], F32R)
        wfh = sb("wfh", [P, C], F32R)
        wfl = sb("wfl", [P, C], F32R)
        rows = sb("rows", [P, 3, CM])
        ind = sb("ind", [P, GQ, GC])
        ones = sb("ones", [P, P])
        bmat = sb("bmat", [P, CM], F32R)
        onesr = sb("onesr", [P, W], F32R)
        ind8 = sb("ind8", [P, GQ])
        bcc = sb("bcc", [P, 1])
        badc = sb("badc", [P, 1])
        bfc = sb("bfc", [P, Q])
        kk9 = sb("kk9", [P, 2, TAPS])
        eps = sb("eps", [P, 2])
        kout = sb("kout", [P, 4])
        bst = sb("bst", [P, Q, NT, 6])
        mv = sb("mv", [P, Q, 2])
        cent = sb("cent", [P, Q, TAPS + 1])
        mx = sb("mx", [P, Q, TAPS])
        negm = sb("negm", [P, Q])
        va = sb("va", [P, 6, Q])
        ggs = sb("ggs", [P, TAPS + 1])
        gk = sb("gk", [P, TAPS])
        sums = sb("sums", [P, Q, PART_SUM[NT]])
        nmean = sb("nmean", [P, Q])
        m2 = sb("m2", [P, Q])
        vb = sb("vb", [P, 3, Q])
        spread = sb("spread", [P, 2, Q, GQ])
        vt = sb("vt", [P, 5, G])
        s_t = sb("s_t", [P, G])
        b_t = sb("b_t", [P, G])

        pac = [bank(f"pac{i}") for i in range(C_BANKS)]
        pb = [bank(f"pb{i}") for i in range(2)]
        pd = [bank(f"pd{i}") for i in range(2)]
        ps = bank("ps")

        const_in = sem("const_in")
        kt_in = sem("kt_in")
        x_in = [sem(f"x_in{c}") for c in range(Q)]
        t_in = [sem(f"t_in{c}") for c in range(Q)]
        x1_out = sem("x1_out")
        stored = [sem(f"stored{c}") for c in range(Q)]
        pool_const = sem("pool_const")
        kmax_all = sem("kmax_all")
        kmax_part = sem("kmax_part")
        vec_const = sem("vec_const")
        dve_const = sem("dve_const")
        dve_prep = sem("dve_prep")
        dve_dyn = sem("dve_dyn")
        dve_stat = sem("dve_stat")
        prep_done = sem("prep_done")
        stat_ready = sem("stat_ready")
        stat_mm = sem("stat_mm")
        stat_mm2 = sem("stat_mm2")
        stat_ready2 = sem("stat_ready2")
        sd_done = sem("sd_done")
        sd2_done = sem("sd2_done")
        negm_done = sem("negm_done")
        wc_done = sem("wc_done")
        dyn_done = sem("dyn_done")
        st_done = sem("st_done")
        mrow_done = sem("mrow_done")
        nmean_done = sem("nmean_done")
        xs_hi = sem("xs_hi")
        xs_lo = sem("xs_lo")
        a_mm = sem("a_mm")
        f_hi = sem("f_hi")
        f_lo = sem("f_lo")
        b_mm = sem("b_mm")
        y_hi = sem("y_hi")
        y_lo = sem("y_lo")
        c_mm = sem("c_mm")
        x1_done = sem("x1_done")
        sq_done = sem("sq_done")
        u_done = sem("u_done")
        hl_hi = sem("hl_hi")
        hl_lo = sem("hl_lo")
        d_mm = sem("d_mm")
        out_done = sem("out_done")

        def f32(ap):
            return ap.bitcast(F32)

        wcs = dtmp[:, 0:Q, :]
        stage = tb[:, :, :, :, :].rearrange("p a j b w -> p (a j b w)").rearrange("p (g m) -> p g m", m=M6)
        stage_flat = tb[:, :, :, :, :].rearrange("p a j b w -> p (a j b w)")
        kh_flat = k_h[:, :, :, :].rearrange("p g t m -> p (g t m)")
        kl_flat = k_l[:, :, :, :].rearrange("p g t m -> p (g t m)")

        def t_slot(c):
            return tb[:, T_SLOT[c], :, :, :]

        def reached(eng, semaphore, value):
            if not isinstance(value, int) or value > 0:
                eng.wait_ge(semaphore, value)

        def images(eng, step):
            step(0, d=False)
            step(1)
            with eng.Fori(2, N - 1) as n:
                step(n)
            step(N - 1, more=False)

        block = ctx.enter_context(nc.Block())

        @block.sync
        def _(sp):
            def load_x(n):
                reached(sp, x1_done, n * X1_OPS)
                for c in range(Q):
                    sp.dma_start(xb[:, c, :], x_d[n, :, c, :]).then_inc(x_in[c], 16)

            def write_x1(n):
                sp.wait_ge(x1_done, (n + 1) * X1_OPS)
                sp.wait_ge(mrow_done, n + 1)
                dst = sc_w[n]
                src = x1b[:, :, :, :, :].rearrange("p q k b w -> p q (k b w)")
                sp.dma_start(dst[:, :, 0:BW], src[:, :, 0:BW]).then_inc(x1_out, 16)
                sp.dma_start(dst[:, :, BW:BW + W], mrow[:, :, :]).then_inc(x1_out, 16)
                sp.dma_start(dst[:, :, BW + W:5 * BW + W], src[:, :, BW:5 * BW]).then_inc(x1_out, 16)
                sp.dma_start(dst[:, :, 5 * BW + W:5 * BW + 2 * W], mrow[:, :, :]).then_inc(x1_out, 16)
                sp.dma_start(dst[:, :, 5 * BW + 2 * W:], src[:, :, 5 * BW:]).then_inc(x1_out, 16)

            def load_t(n, c):
                if c == 0:
                    sp.wait_ge(x1_out, (n + 1) * 80)
                if c == 3:
                    sp.wait_ge(stored[0], (n + 1) * 16)
                else:
                    reached(sp, stored[3 if c == 0 else c], n * 16)
                for p in range(IR):
                    at = {0: 5 * BW + W, 1: 0, 6: 5 * BW + 2 * W, 7: W}.get(p, (p - 1) * BW + W)
                    k = partition_of(p)
                    sp.dma_start(t_slot(c)[k:k + GC].rearrange("c j b w -> c j (b w)"),
                                 sc_r[n, c, :, :, at:at + BW]).then_inc(t_in[c], 16)

            def store(n, c):
                sp.wait_ge(out_done, n * G + (c + 1) * GQ)
                sp.dma_start(out[n, c], t_slot(c)[0:M6].rearrange("p j b w -> p (j b w)")).then_inc(stored[c], 16)

            def d_first(n):
                for c in range(3):
                    load_t(n, c)
                store(n, 0)
                load_t(n, 3)

            def step(n, d=True, more=True):
                if d:
                    d_first(n - 1)
                if more:
                    load_x(n + 1)
                write_x1(n)
                if d:
                    for c in range(1, Q):
                        store(n - 1, c)

            load_x(0)
            for dst, src in ((wc[:, :, :], wct), (dtmp[:, 0:4, :].rearrange("p a b -> p (a b)"), wft),
                             (rows[:, 0, :], wck[0].partition_broadcast(P)), (rows[:, 1, :], wck[1].partition_broadcast(P)),
                             (rows[:, 2, :], bck.partition_broadcast(P)), (kk9[:, 0, :], wkk.partition_broadcast(P)),
                             (kk9[:, 1, :], bkk.partition_broadcast(P)), (bcc[:, :], bc.rearrange("(p a) -> p a", a=1)),
                             (badc[:, :], b_ad.rearrange("(p a) -> p a", a=1)), (bfc[:, :], bf),
                             (dtmp[0:1, Q, :], bc.rearrange("(a p) -> a p", a=1)),
                             (dtmp[32:33, Q, :], bc.rearrange("(a p) -> a p", a=1))):
                sp.dma_start(dst, src).then_inc(const_in, 16)
            sp.wait_ge(vec_const, 1)
            for p in range(IR):
                lo, hi = max(0, p - 2), min(OR_ - 1, p)
                k, at = partition_of(p), 2 - p + lo
                sp.dma_start(stage[k:k + GC, :, lo * GC:(hi + 1) * GC],
                             kt[:, :, at * GC:(at + hi - lo + 1) * GC]).then_inc(kt_in, 16)
            sp.wait_ge(vec_const, 3)
            images(sp, step)
            d_first(N - 1)
            for c in range(1, Q):
                store(N - 1, c)
            for c in range(Q):
                sp.wait_ge(stored[c], N * 16)

        @block.gpsimd
        def _(pool):
            pool.memset(ind[:, :, :], 1.0 / GC).then_inc(pool_const, 1)
            pool.memset(ind8[:, :], 1.0).then_inc(pool_const, 1)
            pool.wait_ge(pool_const, 2)
            for n, (base, mult, step_) in enumerate(((0, 1, -GC), (GC - 1, -1, GC))):
                pool.affine_select(out=ind[:, :, :], in_=ind[:, :, :], compare_op=ALU.is_ge, fill=0.0, base=base,
                                   pattern=[[step_, GQ], [0, GC]], channel_multiplier=mult).then_inc(pool_const, 1)
                pool.affine_select(out=ind8[:, :], in_=ind8[:, :], compare_op=ALU.is_ge, fill=0.0, base=base,
                                   pattern=[[step_, GQ]], channel_multiplier=mult).then_inc(pool_const, 1)
                pool.wait_ge(pool_const, 4 + 2 * n)
            pool.wait_ge(kmax_part, 1)
            pool.partition_all_reduce(kout[:, 1:2], kout[:, 0:1], P, bass.bass_isa.ReduceOp.max).then_inc(kmax_all, 1)

            def d_groups(n, groups):
                for g in groups:
                    pool.wait_ge(hl_hi, n * G + g + 1)
                    pool.tensor_tensor(hl[:, g % HL_RING, 1, :, 1:W + 1], un[:, g % U_RING], hl[:, g % HL_RING, 0, :, 1:W + 1],
                                       ALU.subtract).then_inc(hl_lo, 1)

            def step(n, d=True, more=True):
                if d:
                    d_groups(n - 1, range(G))

            images(pool, step)
            d_groups(N - 1, range(G))

        @block.scalar
        def _(act):
            def d_groups(n, groups):
                for g in groups:
                    if g % GQ == 0:
                        act.wait_ge(t_in[g // GQ], (n + 1) * 16 * IR)
                    if g == 0:
                        act.wait_ge(st_done, n + 1)
                    reached(act, hl_lo, n * G + g - U_RING + 1)
                    act.activation(un[:, g % U_RING], t_slot(g // GQ)[:, g % GQ], ACT.Identity,
                                   bias=b_t[:, g:g + 1], scale=s_t[:, g:g + 1]).then_inc(u_done, 1)
                    act.wait_ge(u_done, n * G + g + 1)
                    reached(act, d_mm, n * G + g - HL_RING + 1)
                    act.activation(hl[:, g % HL_RING, 0, :, 1:W + 1], un[:, g % U_RING], ACT.Copy).then_inc(hl_hi, 1)

            def f_high(n, t):
                r0, nr = TILES[t]
                act.wait_ge(a_mm, n * UNITS + Q * (t + 1))
                if t == 0:
                    reached(act, b_mm, n * NT)
                act.activation(fh[:, r0 + 1:r0 + 1 + nr, 1:W + 1], pac[t % 2][:, 0:nr * W].rearrange("p (r w) -> p r w", w=W),
                               ACT.Relu).then_inc(f_hi, 1)

            def a_phase(n, d):
                for t, (r0, nr) in enumerate(TILES):
                    for c in range(Q):
                        i = t * Q + c
                        if i == 0:
                            act.wait_ge(negm_done, n + 1)
                            reached(act, sq_done, n * Q)
                        reached(act, a_mm, n * UNITS + i - XS_RING + 1)
                        act.activation(xs[:, i % XS_RING, 0, 0:nr * W], xb[:, c, r0 * W:(r0 + nr) * W], ACT.Identity,
                                       bias=negm[:, c:c + 1]).then_inc(xs_hi, 1)
                    if t:
                        f_high(n, t - 1)
                    if d and t == 2:
                        root_second(n - 1)
                if d:
                    d_groups(n - 1, range(EARLY))
                f_high(n, NT - 1)

            def y_high(n, t):
                nr = TILES[t][1]
                act.wait_ge(b_mm, n * NT + t + 1)
                reached(act, c_mm, n * UNITS + Q * (t - 1) if t >= 2 else n * UNITS)
                act.activation(yp[:, t % 2, 0, 0:nr * W], pb[t % 2][:, 0:nr * W], ACT.Identity,
                               bias=badc[:, 0:1]).then_inc(y_hi, 1)

            def square(n, c):
                if c == 0:
                    act.wait_ge(nmean_done, n + 1)
                reached(act, sq_done, n * Q + c)
                act.activation(xs[:, :, :, :].rearrange("p a b m -> p (a b m)")[:, 0:PX], x1b[:, c].rearrange("p k b w -> p (k b w)"),
                               ACT.Square, bias=nmean[:, c:c + 1], accum_out=m2[:, c:c + 1]).then_inc(sq_done, 1)

            def root_first(n):
                act.wait_ge(stat_mm, 3 * n + 2)
                act.activation(va[:, 3, :], ps[:, 8:8 + Q], ACT.Sqrt, bias=eps[:, 0:1]).then_inc(sd_done, 1)

            def root_second(n):
                act.wait_ge(stat_mm2, 2 * n + 2)
                act.activation(vt[:, 0, :], ps[:, 96:96 + G], ACT.Sqrt, bias=eps[:, 1:2],
                               scale=XSCALE ** -2).then_inc(sd2_done, 1)

            def step(n, d=True, more=True):
                a_phase(n, d)
                if d:
                    d_groups(n - 1, range(EARLY, GQ))
                for t in range(NT - 1):
                    y_high(n, t)
                if d:
                    d_groups(n - 1, range(GQ, GQ + EARLY))
                y_high(n, NT - 1)
                at = GQ + EARLY
                for c in range(Q):
                    if d:
                        d_groups(n - 1, range(at, at + 3))
                        at += 3
                    square(n, c)
                if d:
                    d_groups(n - 1, range(at, G))
                if more:
                    root_first(n + 1)

            act.wait_ge(vec_const, 3)
            root_first(0)
            images(act, step)
            root_second(N - 1)
            d_groups(N - 1, range(G))

        @block.vector
        def _(vec):
            def chain(semaphore, n, per_image):
                count = [0]

                def go(ins):
                    count[0] += 1
                    assert count[0] <= per_image
                    ins.then_inc(semaphore, 1)
                    vec.wait_ge(semaphore, n * per_image + count[0])
                return go

            def constants():
                go = chain(dve_const, 0, 8)
                vec.memset(f32(fh[:, :, :]), 0.0)
                vec.memset(f32(fl[:, :, :]), 0.0)
                vec.memset(hl[:, :, :, :, :], 0.0)
                vec.memset(f32(onesr[:, :]), 1.0)
                vec.memset(ones[:, :], 1.0 / GC)
                vec.memset(f32(bmat[:, :]), 0.0)
                vec.memset(eps[:, 0:1], EPS)
                vec.memset(eps[:, 1:2], EPS / XSCALE ** 2)
                vec.memset(stage, 0.0).then_inc(vec_const, 1)
                vec.wait_ge(vec_const, 1)
                vec.wait_ge(const_in, 12 * 16)
                wf32 = dtmp[:, 0:4, :].rearrange("p a b -> p (a b)")
                vec.tensor_copy(bmat[0:1, :], dtmp[0:1, Q, :])
                vec.tensor_copy(bmat[32:33, :], dtmp[32:33, Q, :])
                go(vec.tensor_copy(wfh[:, :], wf32))
                vec.tensor_tensor(wfl[:, :], wf32, f32(wfh[:, :]), ALU.subtract)
                go(vec.tensor_tensor(dtmp[32:33, Q + 1, :], dtmp[32:33, Q, :], f32(bmat[32:33, :]), ALU.subtract))
                go(vec.tensor_copy(bmat[32:33, :], dtmp[32:33, Q + 1, :]))
                vec.wait_ge(kt_in, IR * 16)
                vec.tensor_reduce(kout[:, 0:1], stage_flat, AX.X, ALU.max, apply_absolute_value=True).then_inc(kmax_part, 1)
                vec.wait_ge(kmax_all, 1)
                go(vec.tensor_scalar(kout[:, 3:4], kout[:, 1:2], 1e-30, 1.0 / WSCALE, ALU.max, ALU.mult))
                go(vec.reciprocal(kout[:, 0:1], kout[:, 3:4]))
                go(vec.tensor_scalar(kout[:, 2:3], kout[:, 3:4], 1.0 / XSCALE, None, ALU.mult))
                go(vec.tensor_scalar(kh_flat, stage_flat, kout[:, 0:1], None, ALU.mult))
                vec.scalar_tensor_tensor(out=kl_flat, in0=stage_flat, scalar=kout[:, 0:1], in1=kh_flat,
                                         op0=ALU.mult, op1=ALU.subtract).then_inc(vec_const, 2)

            def inverse_root(out_, sd, half_v, go):
                go(vec.reciprocal(out_, sd))
                go(vec.tensor_tensor(sd, out_, out_, ALU.mult))
                go(vec.tensor_tensor(sd, sd, half_v, ALU.mult))
                return vec.scalar_tensor_tensor(out=out_, in0=sd, scalar=1.5, in1=out_, op0=ALU.add, op1=ALU.mult)

            def prep_pieces(n):
                def stats(c, t):
                    r0, nr = TILES[t]
                    if t == 0:
                        vec.wait_ge(x_in[c], (n + 1) * 16)
                    ins = vec.bn_stats(bst[:, c, t, :], xb[:, c, r0 * W:(r0 + nr) * W])
                    if t == NT - 1:
                        ins.then_inc(prep_done, 1)

                def maxima(c):
                    src = xb[:, c, :].rearrange("p (k r l w) -> p k l r w", k=3, r=PX_BLOCK, l=3)
                    for k in range(3):
                        ins = vec.tensor_reduce(mx[:, c, 3 * k:3 * k + 3], src[:, k], AX.XY, ALU.max)
                    ins.then_inc(prep_done, 1)

                pieces = []
                for c in range(Q):
                    pieces += [(stats, (c, t)) for t in range(NT)] + [(maxima, (c,))]
                return pieces

            def prep_end(n):
                go = chain(dve_prep, n, 8)
                vec.wait_ge(prep_done, 2 * Q * (n + 1))
                vec.tensor_copy(cent[:, :, 0:TAPS], mx[:, :, :])
                for c in range(Q):
                    ins = vec.bn_aggr(mv[:, c, :], bst[:, c].rearrange("p t s -> p (t s)"))
                ins.then_inc(stat_ready, 1)
                vec.wait_ge(stat_mm, 3 * n + 1)
                vec.tensor_scalar(negm[:, :], ps[:, 0:Q], -1.0, None, ALU.mult).then_inc(negm_done, 1)
                vec.wait_ge(negm_done, n + 1)
                go(vec.tensor_tensor(va[:, 0, :], mv[:, :, 0], negm[:, :], ALU.add))
                go(vec.tensor_tensor(va[:, 1, :], va[:, 0, :], va[:, 0, :], ALU.mult))
                vec.tensor_tensor(va[:, 2, :], va[:, 1, :], mv[:, :, 1], ALU.add).then_inc(stat_ready, 1)
                for c in range(Q):
                    vec.tensor_scalar(cent[:, c, 0:TAPS], cent[:, c, 0:TAPS], negm[:, c:c + 1], None, ALU.add)
                vec.tensor_copy(cent[:, :, TAPS], va[:, 0, :])
                vec.wait_ge(sd_done, n + 1)
                go(vec.tensor_scalar(va[:, 4, :], ps[:, 8:8 + Q], EPS, -0.5, ALU.add, ALU.mult))
                go(inverse_root(va[:, 5, :], va[:, 3, :], va[:, 4, :], go))
                for c in range(Q):
                    ins = vec.tensor_scalar(wcs[:, c, :], wc[:, c, :], va[:, 5, c:c + 1], None, ALU.mult)
                ins.then_inc(stat_ready, 1)
                vec.wait_ge(stat_ready, 3 * (n + 1))
                go(vec.tensor_copy(wch[:, :, :], wcs[:, :, :]))
                vec.tensor_tensor(wcl[:, :, :], wcs[:, :, :], f32(wch[:, :, :]), ALU.subtract).then_inc(wc_done, 1)

            def dynamic_kernel(n):
                go = chain(dve_dyn, n, 5)
                vec.wait_ge(stat_mm, 3 * n + 3)
                go(vec.tensor_scalar(ggs[:, :], ps[:, 16:16 + TAPS + 1], bcc[:, 0:1], 0.0, ALU.add, ALU.max))
                go(vec.scalar_tensor_tensor(out=gk[:, :], in0=kk9[:, 0, :], scalar=ggs[:, TAPS:TAPS + 1], in1=kk9[:, 1, :],
                                            op0=ALU.mult, op1=ALU.add))
                for k in range(TAPS):
                    ins = vec.scalar_tensor_tensor(out=dtmp[:, k, :], in0=rows[:, 1, :], scalar=ggs[:, k:k + 1], in1=rows[:, 2, :],
                                                   op0=ALU.mult, op1=ALU.add)
                go(ins)
                for k in range(TAPS):
                    ins = vec.scalar_tensor_tensor(out=dtmp[:, k, :], in0=rows[:, 0, :], scalar=gk[:, k:k + 1], in1=dtmp[:, k, :],
                                                   op0=ALU.mult, op1=ALU.add)
                go(ins)
                go(vec.tensor_scalar(dynh[:, :, :], dtmp[:, :, :], 0.0, None, ALU.max))
                vec.scalar_tensor_tensor(out=dynl[:, :, :], in0=dtmp[:, :, :], scalar=0.0, in1=f32(dynh[:, :, :]),
                                         op0=ALU.max, op1=ALU.subtract).then_inc(dyn_done, 1)

            STAT_LINKS = 9
            def x1_means(n):
                vec.wait_ge(x1_done, (n + 1) * X1_OPS)
                vec.tensor_reduce(vb[:, 0, :], sums[:, :, :], AX.X, ALU.add).then_inc(dve_stat, 1)
                vec.wait_ge(dve_stat, STAT_LINKS * n + 1)
                vec.tensor_scalar(nmean[:, :], vb[:, 0, :], -1.0 / PX, None, ALU.mult).then_inc(nmean_done, 1)

            def x1_group_means(n):
                vec.wait_ge(stat_mm2, 2 * n + 1)
                reached(vec, x1_out, n * 80)
                vec.tensor_scalar(mrow[:, :, :], ps[:, 32:32 + Q].unsqueeze(2).to_broadcast([P, Q, W]), -1.0, None,
                                  ALU.mult).then_inc(mrow_done, 1)
                vec.tensor_tensor(vb[:, 1, :], ps[:, 32:32 + Q], nmean[:, :], ALU.subtract).then_inc(dve_stat, 1)
                vec.wait_ge(dve_stat, STAT_LINKS * n + 2)
                vec.tensor_tensor(vb[:, 2, :], vb[:, 1, :], vb[:, 1, :], ALU.mult).then_inc(dve_stat, 1)

            def x1_variances(n):
                vec.wait_ge(sq_done, (n + 1) * Q)
                vec.wait_ge(dve_stat, STAT_LINKS * n + 3)
                vec.scalar_tensor_tensor(out=vb[:, 0, :], in0=m2[:, :], scalar=1.0 / PX, in1=vb[:, 2, :],
                                         op0=ALU.mult, op1=ALU.add).then_inc(dve_stat, 1)
                vec.wait_ge(dve_stat, STAT_LINKS * n + 4)
                mask = ind8[:, :].unsqueeze(1).to_broadcast([P, Q, GQ])
                vec.tensor_tensor(spread[:, 0], nmean[:, :].unsqueeze(2).to_broadcast([P, Q, GQ]), mask, ALU.mult)
                vec.tensor_tensor(spread[:, 1], vb[:, 0, :].unsqueeze(2).to_broadcast([P, Q, GQ]), mask,
                                  ALU.mult).then_inc(stat_ready2, 1)

            def x1_scales(n):
                vec.wait_ge(sd2_done, n + 1)
                vec.tensor_scalar(vt[:, 1, :], ps[:, 96:96 + G], -0.5 * XSCALE ** -2, -0.5 * EPS * XSCALE ** -2, ALU.mult,
                                  ALU.add).then_inc(dve_stat, 1)
                vec.wait_ge(dve_stat, STAT_LINKS * n + 5)
                at = [5]

                def go(ins):
                    at[0] += 1
                    ins.then_inc(dve_stat, 1)
                    vec.wait_ge(dve_stat, STAT_LINKS * n + at[0])
                reached(vec, u_done, n * G)
                go(inverse_root(s_t[:, :], vt[:, 0, :], vt[:, 1, :], go))
                vec.tensor_tensor(b_t[:, :], ps[:, 64:64 + G], s_t[:, :], ALU.mult).then_inc(st_done, 1)
                assert at[0] == STAT_LINKS

            def x_low(n, i):
                t, c = divmod(i, Q)
                r0, nr = TILES[t]
                vec.wait_ge(xs_hi, n * UNITS + i + 1)
                vec.scalar_tensor_tensor(out=xs[:, i % XS_RING, 1, 0:nr * W], in0=xb[:, c, r0 * W:(r0 + nr) * W],
                                         scalar=negm[:, c:c + 1], in1=f32(xs[:, i % XS_RING, 0, 0:nr * W]),
                                         op0=ALU.add, op1=ALU.subtract).then_inc(xs_lo, 1)

            def f_low(n, t):
                r0, nr = TILES[t]
                vec.wait_ge(f_hi, n * NT + t + 1)
                vec.scalar_tensor_tensor(out=fl[:, r0 + 1:r0 + 1 + nr, 1:W + 1],
                                         in0=pac[t % 2][:, 0:nr * W].rearrange("p (r w) -> p r w", w=W), scalar=0.0,
                                         in1=f32(fh[:, r0 + 1:r0 + 1 + nr, 1:W + 1]), op0=ALU.max,
                                         op1=ALU.subtract).then_inc(f_lo, 1)

            def y_low(n, t):
                nr = TILES[t][1]
                vec.wait_ge(y_hi, n * NT + t + 1)
                vec.scalar_tensor_tensor(out=yp[:, t % 2, 1, 0:nr * W], in0=pb[t % 2][:, 0:nr * W], scalar=badc[:, 0:1],
                                         in1=f32(yp[:, t % 2, 0, 0:nr * W]), op0=ALU.add,
                                         op1=ALU.subtract).then_inc(y_lo, 1)

            def residual(n, t):
                if t == 0:
                    reached(vec, x1_out, n * 80)
                for c in range(Q):
                    vec.wait_ge(c_mm, n * UNITS + t * Q + c + 1)
                    acc = pac[(t * Q + c) % C_BANKS]
                    r0 = TILES[t][0]
                    for j, (r, m) in enumerate(PARTS[t]):
                        k, b = r % OR_, r // OR_
                        vec.scalar_tensor_tensor(
                            out=x1b[:, c, k:k + m, b, :], in0=acc[:, (r - r0) * W:(r - r0 + m) * W].rearrange("p (r w) -> p r w", w=W),
                            scalar=bfc[:, c:c + 1], in1=xb[:, c, r * W:(r + m) * W].rearrange("p (r w) -> p r w", w=W),
                            op0=ALU.add, op1=ALU.add,
                            accum_out=sums[:, c, PART_SUM[t] + j:PART_SUM[t] + j + 1]).then_inc(x1_done, 1)

            def output(n, g):
                vec.wait_ge(d_mm, n * G + g + 1)
                dst = t_slot(g // GQ)[0:M6, g % GQ]
                vec.scalar_tensor_tensor(out=dst, in0=pd[g % 2][0:M6, 0:BW].rearrange("p (b w) -> p b w", w=W),
                                         scalar=kout[0:M6, 2:3], in1=dst, op0=ALU.mult, op1=ALU.add).then_inc(out_done, 1)

            def step(n, d=True, more=True):
                for t in range(NT):
                    for c in range(Q):
                        x_low(n, t * Q + c)
                    if t:
                        f_low(n, t - 1)
                    if d and t == 0:
                        x1_variances(n - 1)
                    if d and t == 2:
                        x1_scales(n - 1)
                f_low(n, NT - 1)
                dynamic_kernel(n)
                if d:
                    for g in range(GQ):
                        output(n - 1, g)
                y_low(n, 0)
                for t in range(1, NT):
                    y_low(n, t)
                    residual(n, t - 1)
                residual(n, NT - 1)
                x1_means(n)
                pieces = prep_pieces(n + 1) if more else []
                if not d:
                    x1_group_means(n)
                for g in range(GQ, G) if d else ():
                    output(n - 1, g)
                    if g == GQ + EARLY:
                        x1_group_means(n)
                    if g >= GQ + 4:
                        for what, args in pieces[:(2 if g % 4 == 0 else 1)]:
                            what(*args)
                        pieces = pieces[(2 if g % 4 == 0 else 1):]
                for what, args in pieces:
                    what(*args)
                if more:
                    prep_end(n + 1)

            constants()
            vec.wait_ge(pool_const, 6)
            for what, args in prep_pieces(0):
                what(*args)
            prep_end(0)
            images(vec, step)
            x1_variances(N - 1)
            x1_scales(N - 1)
            for g in range(G):
                output(N - 1, g)

        @block.tensor
        def _(pe):
            def three(acc, high_w, low_w, high_x, low_x, start, stop):
                pe.matmul(acc, high_w, high_x, start=start, stop=False)
                pe.matmul(acc, high_w, low_x, start=False, stop=False)
                return pe.matmul(acc, low_w, high_x, start=False, stop=stop)

            def a_tile(n, t):
                nr = TILES[t][1]
                if t >= 2:
                    pe.wait_ge(f_lo, n * NT + t - 1)
                acc = pac[t % 2][:, 0:nr * W]
                pe.matmul(acc.rearrange("p (r w) -> p r w", w=W), bmat[:, :], onesr[:, :].unsqueeze(1).to_broadcast([P, nr, W]),
                          start=True, stop=False)
                for c in range(Q):
                    i = t * Q + c
                    pe.wait_ge(xs_lo, n * UNITS + i + 1)
                    three(acc, wch[:, c, :], wcl[:, c, :], xs[:, i % XS_RING, 0, 0:nr * W], xs[:, i % XS_RING, 1, 0:nr * W],
                          False, c == Q - 1).then_inc(a_mm, 1)

            def b_tile(n, t):
                r0, nr = TILES[t]
                pe.wait_ge(f_lo, n * NT + min(t + 2, NT))
                reached(pe, y_lo, n * NT + t - 1 if t >= 2 else n * NT)
                acc = pb[t % 2][:, 0:nr * W].rearrange("p (r w) -> p r w", w=W)
                for k in range(TAPS):
                    dy, dx = divmod(k, 3)
                    ins = three(acc, dynh[:, k, :], dynl[:, k, :], fh[:, r0 + dy:r0 + dy + nr, dx:dx + W],
                                fl[:, r0 + dy:r0 + dy + nr, dx:dx + W], k == 0, k == TAPS - 1)
                ins.then_inc(b_mm, 1)

            def c_tile(n, t):
                nr = TILES[t][1]
                pe.wait_ge(y_lo, n * NT + t + 1)
                for c in range(Q):
                    i = t * Q + c
                    if i >= C_BANKS:
                        j = i - C_BANKS
                        pe.wait_ge(x1_done, n * X1_OPS + x1_count(j // Q, j % Q))
                    three(pac[i % C_BANKS][:, 0:nr * W], wfh[:, c * P:(c + 1) * P], wfl[:, c * P:(c + 1) * P],
                          yp[:, t % 2, 0, 0:nr * W], yp[:, t % 2, 1, 0:nr * W], True, True).then_inc(c_mm, 1)

            def d_group(n, g):
                pe.wait_ge(hl_lo, n * G + g + 1)
                reached(pe, out_done, n * G + g - 1)
                acc = pd[g % 2][0:M6, 0:BW].rearrange("p (b w) -> p b w", w=W)
                s = g % HL_RING
                for dx in range(3):
                    ins = three(acc, k_h[:, g, dx, :], k_l[:, g, dx, :], hl[:, s, 0, :, dx:dx + W], hl[:, s, 1, :, dx:dx + W],
                                dx == 0, dx == 2)
                ins.then_inc(d_mm, 1)

            def group_sums(n):
                pe.wait_ge(stat_ready, 3 * n + 1)
                pe.matmul(ps[:, 0:Q], ind_m, mv[:, :, 0], start=True, stop=True).then_inc(stat_mm, 1)
                pe.wait_ge(stat_ready, 3 * n + 2)
                pe.matmul(ps[:, 8:8 + Q], ind_m, va[:, 2, :], start=True, stop=True).then_inc(stat_mm, 1)

            def kernel_inputs(n):
                pe.wait_ge(stat_ready, 3 * n + 3)
                for c in range(Q):
                    ins = pe.matmul(ps[:, 16:16 + TAPS + 1], wcs[:, c, :], cent[:, c, :], start=c == 0, stop=c == Q - 1)
                ins.then_inc(stat_mm, 1)

            def x1_group_means(n):
                pe.wait_ge(nmean_done, n + 1)
                pe.matmul(ps[:, 32:32 + Q], ind_m, nmean[:, :], start=True, stop=True).then_inc(stat_mm2, 1)

            def x1_spread(n):
                pe.wait_ge(stat_ready2, n + 1)
                pe.matmul(ps[:, 64:64 + 2 * G], ones[:, :], spread[:, :, :, :].rearrange("p a q j -> p (a q j)"),
                          start=True, stop=True).then_inc(stat_mm2, 1)

            def step(n, d=True, more=True):
                pe.wait_ge(wc_done, n + 1)
                reached(pe, x1_done, n * X1_OPS)
                for t in range(NT):
                    a_tile(n, t)
                    if d and t == 1:
                        x1_spread(n - 1)
                kernel_inputs(n)
                if d:
                    for g in range(GQ):
                        d_group(n - 1, g)
                pe.wait_ge(dyn_done, n + 1)
                b_tile(n, 0)
                for t in range(1, NT):
                    b_tile(n, t)
                    c_tile(n, t - 1)
                c_tile(n, NT - 1)
                if not d:
                    x1_group_means(n)
                for g in range(GQ, G) if d else ():
                    d_group(n - 1, g)
                    if g == GQ + 2:
                        x1_group_means(n)
                if more:
                    group_sums(n + 1)

            ind_m = ind[:, :, :].rearrange("p j c -> p (j c)")
            pe.wait_ge(pool_const, 6)
            pe.wait_ge(vec_const, 3)
            group_sums(0)
            images(pe, step)
            x1_spread(N - 1)
            for g in range(G):
                d_group(N - 1, g)


INPUTS = ["x", "wct", "bc", "wkk", "bkk", "wck", "bck", "b_ad", "wft", "bf", "kt"]


def kernel(x, L0_conv_Wc, L0_conv_bc, L0_conv_Wkk, L0_conv_bkk, L0_conv_Wck, L0_conv_bck, L0_conv_b_ad, L0_conv_Wf,
           L0_conv_bf, L1_conv_kernels):
    import numpy as np
    from concourse import bacc
    from concourse.bass_utils import run_bass_kernel_spmd

    laid_out = {
        "x": np.asarray(x),
        "wct": np.asarray(L0_conv_Wc).reshape(CM, Q, P).transpose(2, 1, 0),
        "bc": np.asarray(L0_conv_bc),
        "wkk": np.asarray(L0_conv_Wkk),
        "bkk": np.asarray(L0_conv_bkk),
        "wck": np.asarray(L0_conv_Wck).T,
        "bck": np.asarray(L0_conv_bck),
        "b_ad": np.asarray(L0_conv_b_ad),
        "wft": np.asarray(L0_conv_Wf).T,
        "bf": np.asarray(L0_conv_bf).reshape(Q, P).T,
        "kt": np.asarray(L1_conv_kernels).reshape(G, GC, GC, 3, 3).transpose(2, 0, 4, 3, 1)[:, :, :, ::-1, :].reshape(GC, G * 3, 3 * GC),
    }
    nc = bacc.Bacc("TRN2", target_bir_lowering=False, num_devices=1, dynamic_dma_scratch_size=1024)
    arrays, aps = {}, {}
    for name in INPUTS:
        a = np.ascontiguousarray(laid_out[name])
        arrays[name] = a
        aps[name] = nc.dram_tensor(name, a.shape, mybir.dt.from_np(a.dtype), kind="ExternalInput").ap()
    out = nc.dram_tensor("out", (N, Q, M6, GQ * BW), F32, kind="ExternalOutput").ap()
    build(nc, *[aps[name] for name in INPUTS], out)
    r = run_bass_kernel_spmd(nc, [arrays], core_ids=[0])
    got = r.results[0]["out"].reshape(N, Q, OR_, GC, GQ, NB, W)
    return np.ascontiguousarray(got.transpose(0, 1, 4, 3, 5, 2, 6)).reshape(N, C, H, W)
```

```python
from contextlib import ExitStack

import concourse.bass as bass
from concourse import mybir

F32 = mybir.dt.float32
F32R = mybir.dt.float32r
F16 = mybir.dt.float16
ALU = mybir.AluOpType
ACT = mybir.ActivationFunctionType
AX = mybir.AxisListType

P = 128
N, C, H, W = 32, 512, 48, 48
Q = C // P
PX = H * W
CM = 128
TAPS = 9
GC = 16
GQ = P // GC
G = C // GC
OR_ = 6
IR = OR_ + 2
NB = H // OR_
M6 = OR_ * GC
BW = NB * W
SLOTS = H + 2
TILES = [(0, 10), (10, 10), (20, 10), (30, 10), (40, 8)]
NT = len(TILES)
MAXW = 480
UNITS = NT * Q
EPS = 1e-5
XSCALE = 256.0
WSCALE = 8192.0

XS_RING, HL_RING, U_RING = 5, 4, 2
C_BANKS = 3
C_AFTER = (2, 4, 6, 8)
D_FIRST = 10
PREP_AT = (3, 4, 5, 6)
PREP_IN_B = ((2, 3, 4), (5, 6), (7, 8), (9, 10), (11,))
EARLY = 3
AT_SUMS = (13, 15)
AT_MEANS = 12
AT_ROOT, AT_SCALED = 18, 17
AT_SQUARES = (14, 20, 23, 27)
AT_VARIANCES = 30
CELL = 16
BANDS = H // CELL
BAND = CELL * W
PIECES = Q * BANDS
STAGES = 4
HALF = BAND // 2


def row_parts(r0, rows):
    out, r = [], r0
    while r < r0 + rows:
        e = min(r0 + rows, (r // OR_ + 1) * OR_)
        out.append((r, e - r))
        r = e
    return out


PARTS = [row_parts(r0, rows) for r0, rows in TILES]
PART_SUM = [sum(len(p) for p in PARTS[:t]) for t in range(NT + 1)]
X1_OPS = Q * PART_SUM[NT]


def x1_count(t, c):
    return Q * PART_SUM[t] + (c + 1) * len(PARTS[t])


def partition_of(p):
    return GC * {0: 6, 7: 7}.get(p, p - 1)


T_SLOT = [0, 1, 0, 1]


def build(nc, x, wct, bc, wkk, bkk, wck, bck, b_ad, wft, bf, kt, out):
    x_d = x.rearrange("n (q p) h w -> n p q (h w)", q=Q)
    scratch = nc.dram_tensor("x1_rows", (N, C, SLOTS, W), F32, kind="Internal").ap()
    sc_w = scratch.rearrange("n (q p) s w -> n p q (s w)", q=Q)
    sc_r = scratch.rearrange("n (q j c) s w -> n q c j (s w)", q=Q, c=GC)

    with ExitStack() as ctx:
        def sb(name, shape, dt=F32):
            return ctx.enter_context(nc.sbuf_tensor(name, shape, dt))

        def bank(name):
            return ctx.enter_context(nc.psum_tensor(name, [P, 512], F32))

        def sem(name):
            return ctx.enter_context(nc.semaphore(name))

        xb = sb("xb", [P, Q, PX])
        x1b = sb("x1b", [P, Q, OR_, NB, W])
        mrow = sb("mrow", [P, Q, W])
        tb = sb("tb", [P, 3, GQ, NB, W])
        fh = sb("fh", [P, H + 2, W + 2], F32R)
        fl = sb("fl", [P, H + 2, W + 2], F32R)
        k_h = sb("k_h", [P, G, 3, M6], F16)
        k_l = sb("k_l", [P, G, 3, M6], F16)
        xs = sb("xs", [P, XS_RING, 2, MAXW], F32R)
        hl = sb("hl", [P, HL_RING, 2, NB, W + 2], F16)
        un = sb("un", [P, U_RING, NB, W])
        dynh = sb("dynh", [P, TAPS, CM], F32R)
        dynl = sb("dynl", [P, TAPS, CM], F32R)
        dtmp = sb("dtmp", [P, TAPS, CM])
        wc = sb("wc", [P, Q, CM])
        wch = sb("wch", [P, Q, CM], F32R)
        wcl = sb("wcl", [P, Q, CM], F32R)
        wfh = sb("wfh", [P, C], F32R)
        wfl = sb("wfl", [P, C], F32R)
        rows = sb("rows", [P, 3, CM])
        ind = sb("ind", [P, GQ, GC])
        ones = sb("ones", [P, P])
        bmat = sb("bmat", [P, CM], F32R)
        onesr = sb("onesr", [P, W], F32R)
        ind8 = sb("ind8", [P, GQ])
        bcc = sb("bcc", [P, 1])
        badc = sb("badc", [P, 1])
        bfc = sb("bfc", [P, Q])
        kk9 = sb("kk9", [P, 2, TAPS])
        eps = sb("eps", [P, 2])
        kout = sb("kout", [P, 4])
        bst = sb("bst", [P, Q, 2 * BANDS, 6])
        mv = sb("mv", [P, Q, 2])
        cent = sb("cent", [P, Q, TAPS + 1])
        mx = sb("mx", [P, Q, TAPS])
        negm = sb("negm", [P, Q])
        va = sb("va", [P, 6, Q])
        ggs = sb("ggs", [P, TAPS + 1])
        gk = sb("gk", [P, TAPS])
        sums = sb("sums", [P, Q, PART_SUM[NT]])
        nmean = sb("nmean", [P, Q])
        m2 = sb("m2", [P, Q])
        vb = sb("vb", [P, 3, Q])
        spread = sb("spread", [P, 2, Q, GQ])
        vt = sb("vt", [P, 5, G])
        s_t = sb("s_t", [P, G])
        b_t = sb("b_t", [P, G])

        pac = [bank(f"pac{i}") for i in range(C_BANKS)]
        pb = [bank(f"pb{i}") for i in range(2)]
        pd = [bank(f"pd{i}") for i in range(2)]
        ps = bank("ps")

        const_in = sem("const_in")
        kt_in = sem("kt_in")
        x_in = [sem(f"x_in{c}") for c in range(Q)]
        t_in = [sem(f"t_in{c}") for c in range(Q)]
        staged = [sem(f"staged{i}") for i in range(STAGES)]
        x1_out = sem("x1_out")
        stored = [sem(f"stored{c}") for c in range(Q)]
        pool_const = sem("pool_const")
        kmax_all = sem("kmax_all")
        kmax_part = sem("kmax_part")
        vec_const = sem("vec_const")
        dve_const = sem("dve_const")
        dve_prep = sem("dve_prep")
        dve_dyn = sem("dve_dyn")
        dve_stat = sem("dve_stat")
        prep_done = sem("prep_done")
        stat_ready = sem("stat_ready")
        cent_done = sem("cent_done")
        dyn_sum = sem("dyn_sum")
        dyn_hi = sem("dyn_hi")
        stat_mm = sem("stat_mm")
        stat_mm2 = sem("stat_mm2")
        stat_ready2 = sem("stat_ready2")
        sd_done = sem("sd_done")
        sd2_done = sem("sd2_done")
        negm_done = sem("negm_done")
        wc_done = sem("wc_done")
        dyn_done = sem("dyn_done")
        st_done = sem("st_done")
        mrow_done = sem("mrow_done")
        nmean_done = sem("nmean_done")
        xs_hi = sem("xs_hi")
        xs_lo = sem("xs_lo")
        a_mm = sem("a_mm")
        f_hi = sem("f_hi")
        f_lo = sem("f_lo")
        b_mm = sem("b_mm")
        y_hi = sem("y_hi")
        y_lo = sem("y_lo")
        c_mm = sem("c_mm")
        x1_done = sem("x1_done")
        sq_done = sem("sq_done")
        u_done = sem("u_done")
        hl_hi = sem("hl_hi")
        hl_lo = sem("hl_lo")
        d_mm = sem("d_mm")
        out_done = sem("out_done")

        def f32(ap):
            return ap.bitcast(F32)

        wcs = dtmp[:, 0:Q, :]
        stage = tb[:, :, :, :, :].rearrange("p a j b w -> p (a j b w)").rearrange("p (g m) -> p g m", m=M6)
        stage_flat = tb[:, :, :, :, :].rearrange("p a j b w -> p (a j b w)")
        kh_flat = k_h[:, :, :, :].rearrange("p g t m -> p (g t m)")
        kl_flat = k_l[:, :, :, :].rearrange("p g t m -> p (g t m)")

        x_stage = stage_flat[:, 2 * GQ * BW:].rearrange("p (s m) -> p s m", s=STAGES)

        def t_slot(c):
            return tb[:, T_SLOT[c], :, :, :]

        def reached(eng, semaphore, value):
            if not isinstance(value, int) or value > 0:
                eng.wait_ge(semaphore, value)

        def images(eng, step):
            step(0, d=False)
            step(1)
            with eng.Fori(2, N - 1) as n:
                step(n)
            step(N - 1, more=False)

        block = ctx.enter_context(nc.Block())

        @block.sync
        def _(sp):
            def load_x(n, c):
                reached(sp, x1_done, (n - 1) * X1_OPS + x1_count(NT - 1, c) if not isinstance(n, int) or n else 0)
                sp.dma_start(xb[:, c, :], x_d[n, :, c, :]).then_inc(x_in[c], 16)

            def stage_x(n, pieces):
                for i in pieces:
                    c, band = divmod(i, BANDS)
                    sp.wait_ge(prep_done, PIECES * n + i - STAGES + 1 if i >= STAGES else PIECES * n)
                    sp.dma_start(x_stage[:, i % STAGES, :], x_d[n, :, c, band * BAND:(band + 1) * BAND]).then_inc(staged[i % STAGES], 16)

            def write_x1(n):
                sp.wait_ge(x1_done, (n + 1) * X1_OPS)
                sp.wait_ge(mrow_done, n + 1)
                dst = sc_w[n]
                src = x1b[:, :, :, :, :].rearrange("p q k b w -> p q (k b w)")
                sp.dma_start(dst[:, :, 0:BW], src[:, :, 0:BW]).then_inc(x1_out, 16)
                sp.dma_start(dst[:, :, BW:BW + W], mrow[:, :, :]).then_inc(x1_out, 16)
                sp.dma_start(dst[:, :, BW + W:5 * BW + W], src[:, :, BW:5 * BW]).then_inc(x1_out, 16)
                sp.dma_start(dst[:, :, 5 * BW + W:5 * BW + 2 * W], mrow[:, :, :]).then_inc(x1_out, 16)
                sp.dma_start(dst[:, :, 5 * BW + 2 * W:], src[:, :, 5 * BW:]).then_inc(x1_out, 16)

            def load_t(n, c):
                if c == 0:
                    sp.wait_ge(x1_out, (n + 1) * 80)
                reached(sp, stored[(c + 2) % Q], (n + 1 if c >= 2 else n) * 16)
                for p in range(IR):
                    at = {0: 5 * BW + W, 1: 0, 6: 5 * BW + 2 * W, 7: W}.get(p, (p - 1) * BW + W)
                    k = partition_of(p)
                    sp.dma_start(t_slot(c)[k:k + GC].rearrange("c j b w -> c j (b w)"),
                                 sc_r[n, c, :, :, at:at + BW]).then_inc(t_in[c], 16)

            def store(n, c):
                sp.wait_ge(out_done, n * G + (c + 1) * GQ)
                sp.dma_start(out[n, c], t_slot(c)[0:M6].rearrange("p j b w -> p (j b w)")).then_inc(stored[c], 16)

            def step(n, d=True, more=True):
                if d:
                    load_t(n - 1, 1)
                if more:
                    stage_x(n + 1, range(STAGES))
                if d:
                    store(n - 1, 0)
                    load_t(n - 1, 2)
                if more:
                    stage_x(n + 1, range(STAGES, PIECES))
                    for c in range(Q - 1):
                        load_x(n + 1, c)
                if d:
                    store(n - 1, 1)
                    load_t(n - 1, 3)
                if more:
                    load_x(n + 1, Q - 1)
                write_x1(n)
                if d:
                    store(n - 1, 2)
                load_t(n, 0)
                if d:
                    store(n - 1, 3)

            for c in range(Q):
                load_x(0, c)
            for dst, src in ((wc[:, :, :], wct), (dtmp[:, 0:4, :].rearrange("p a b -> p (a b)"), wft),
                             (rows[:, 0, :], wck[0].partition_broadcast(P)), (rows[:, 1, :], wck[1].partition_broadcast(P)),
                             (rows[:, 2, :], bck.partition_broadcast(P)), (kk9[:, 0, :], wkk.partition_broadcast(P)),
                             (kk9[:, 1, :], bkk.partition_broadcast(P)), (bcc[:, :], bc.rearrange("(p a) -> p a", a=1)),
                             (badc[:, :], b_ad.rearrange("(p a) -> p a", a=1)), (bfc[:, :], bf),
                             (dtmp[0:1, Q, :], bc.rearrange("(a p) -> a p", a=1)),
                             (dtmp[32:33, Q, :], bc.rearrange("(a p) -> a p", a=1))):
                sp.dma_start(dst, src).then_inc(const_in, 16)
            sp.wait_ge(vec_const, 1)
            for p in range(IR):
                lo, hi = max(0, p - 2), min(OR_ - 1, p)
                k, at = partition_of(p), 2 - p + lo
                sp.dma_start(stage[k:k + GC, :, lo * GC:(hi + 1) * GC],
                             kt[:, :, at * GC:(at + hi - lo + 1) * GC]).then_inc(kt_in, 16)
            sp.wait_ge(vec_const, 3)
            images(sp, step)
            load_t(N - 1, 1)
            store(N - 1, 0)
            load_t(N - 1, 2)
            store(N - 1, 1)
            load_t(N - 1, 3)
            store(N - 1, 2)
            store(N - 1, 3)
            for c in range(Q):
                sp.wait_ge(stored[c], N * 16)

        @block.gpsimd
        def _(pool):
            pool.memset(ind[:, :, :], 1.0 / GC).then_inc(pool_const, 1)
            pool.memset(ind8[:, :], 1.0).then_inc(pool_const, 1)
            pool.wait_ge(pool_const, 2)
            for n, (base, mult, step_) in enumerate(((0, 1, -GC), (GC - 1, -1, GC))):
                pool.affine_select(out=ind[:, :, :], in_=ind[:, :, :], compare_op=ALU.is_ge, fill=0.0, base=base,
                                   pattern=[[step_, GQ], [0, GC]], channel_multiplier=mult).then_inc(pool_const, 1)
                pool.affine_select(out=ind8[:, :], in_=ind8[:, :], compare_op=ALU.is_ge, fill=0.0, base=base,
                                   pattern=[[step_, GQ]], channel_multiplier=mult).then_inc(pool_const, 1)
                pool.wait_ge(pool_const, 4 + 2 * n)
            pool.wait_ge(kmax_part, 1)
            pool.partition_all_reduce(kout[:, 1:2], kout[:, 0:1], P, bass.bass_isa.ReduceOp.max).then_inc(kmax_all, 1)

            def d_groups(n, groups):
                for g in groups:
                    pool.wait_ge(hl_hi, n * G + g + 1)
                    pool.tensor_tensor(hl[:, g % HL_RING, 1, :, 1:W + 1], un[:, g % U_RING], hl[:, g % HL_RING, 0, :, 1:W + 1],
                                       ALU.subtract).then_inc(hl_lo, 1)

            def step(n, d=True, more=True):
                if d:
                    d_groups(n - 1, range(G))

            images(pool, step)
            d_groups(N - 1, range(G))

        @block.scalar
        def _(act):
            def d_groups(n, groups):
                for g in groups:
                    if g % GQ == 0:
                        act.wait_ge(t_in[g // GQ], (n + 1) * 16 * IR)
                    if g == 0:
                        act.wait_ge(st_done, n + 1)
                    reached(act, hl_lo, n * G + g - U_RING + 1)
                    act.activation(un[:, g % U_RING], t_slot(g // GQ)[:, g % GQ], ACT.Identity,
                                   bias=b_t[:, g:g + 1], scale=s_t[:, g:g + 1]).then_inc(u_done, 1)
                    act.wait_ge(u_done, n * G + g + 1)
                    reached(act, d_mm, n * G + g - HL_RING + 1)
                    act.activation(hl[:, g % HL_RING, 0, :, 1:W + 1], un[:, g % U_RING], ACT.Copy).then_inc(hl_hi, 1)

            def f_high(n, t):
                r0, nr = TILES[t]
                act.wait_ge(a_mm, n * UNITS + Q * (t + 1))
                if t == 0:
                    reached(act, b_mm, n * NT)
                act.activation(fh[:, r0 + 1:r0 + 1 + nr, 1:W + 1], pac[t % 2][:, 0:nr * W].rearrange("p (r w) -> p r w", w=W),
                               ACT.Relu).then_inc(f_hi, 1)

            def a_phase(n, d):
                for t, (r0, nr) in enumerate(TILES):
                    for c in range(Q):
                        i = t * Q + c
                        if i == 0:
                            act.wait_ge(negm_done, n + 1)
                            reached(act, sq_done, n * Q)
                        if t == 0:
                            act.wait_ge(x_in[c], (n + 1) * 16)
                        reached(act, a_mm, n * UNITS + i - XS_RING + 1)
                        act.activation(xs[:, i % XS_RING, 0, 0:nr * W], xb[:, c, r0 * W:(r0 + nr) * W], ACT.Identity,
                                       bias=negm[:, c:c + 1]).then_inc(xs_hi, 1)
                    if t:
                        f_high(n, t - 1)
                    if d and t == 1:
                        root_second(n - 1)
                if d:
                    d_groups(n - 1, range(EARLY))
                f_high(n, NT - 1)

            def y_high(n, t):
                nr = TILES[t][1]
                act.wait_ge(b_mm, n * NT + t + 1)
                reached(act, c_mm, n * UNITS + Q * (t - 1) if t >= 2 else n * UNITS)
                act.activation(xs[:, t % 2, 0, 0:nr * W], pb[t % 2][:, 0:nr * W], ACT.Identity,
                               bias=badc[:, 0:1]).then_inc(y_hi, 1)

            def square(n, c):
                if c == 0:
                    act.wait_ge(nmean_done, n + 1)
                reached(act, sq_done, n * Q + c)
                act.activation(xs[:, :, :, :].rearrange("p a b m -> p (a b m)")[:, 0:PX], x1b[:, c].rearrange("p k b w -> p (k b w)"),
                               ACT.Square, bias=nmean[:, c:c + 1], accum_out=m2[:, c:c + 1]).then_inc(sq_done, 1)

            def root_first(n):
                act.wait_ge(stat_mm, 3 * n + 2)
                act.activation(va[:, 3, :], ps[:, 8:8 + Q], ACT.Sqrt, bias=eps[:, 0:1]).then_inc(sd_done, 1)

            def root_second(n):
                act.wait_ge(stat_mm2, 2 * n + 2)
                act.activation(vt[:, 0, :], ps[:, 96:96 + G], ACT.Sqrt, bias=eps[:, 1:2],
                               scale=XSCALE ** -2).then_inc(sd2_done, 1)

            def step(n, d=True, more=True):
                a_phase(n, d)
                if d:
                    d_groups(n - 1, range(EARLY, D_FIRST))
                act.wait_ge(dyn_sum, n + 1)
                act.activation(dynh[:, :, :], dtmp[:, :, :], ACT.Relu).then_inc(dyn_hi, 1)
                for t in range(NT - 1):
                    y_high(n, t)
                if d:
                    d_groups(n - 1, range(D_FIRST, D_FIRST + EARLY))
                y_high(n, NT - 1)
                if d:
                    for g in range(D_FIRST + EARLY, G):
                        d_groups(n - 1, [g])
                        if g == AT_ROOT and more:
                            root_first(n + 1)
                        if g in AT_SQUARES:
                            square(n, AT_SQUARES.index(g))
                else:
                    root_first(n + 1)
                    for c in range(Q):
                        square(n, c)

            act.wait_ge(vec_const, 3)
            root_first(0)
            images(act, step)
            root_second(N - 1)
            d_groups(N - 1, range(G))

        @block.vector
        def _(vec):
            def chain(semaphore, n, per_image):
                count = [0]

                def go(ins):
                    count[0] += 1
                    assert count[0] <= per_image
                    ins.then_inc(semaphore, 1)
                    vec.wait_ge(semaphore, n * per_image + count[0])
                return go

            def constants():
                go = chain(dve_const, 0, 8)
                vec.memset(f32(fh[:, :, :]), 0.0)
                vec.memset(f32(fl[:, :, :]), 0.0)
                vec.memset(hl[:, :, :, :, :], 0.0)
                vec.memset(f32(onesr[:, :]), 1.0)
                vec.memset(ones[:, :], 1.0 / GC)
                vec.memset(f32(bmat[:, :]), 0.0)
                vec.memset(eps[:, 0:1], EPS)
                vec.memset(eps[:, 1:2], EPS / XSCALE ** 2)
                vec.memset(stage, 0.0).then_inc(vec_const, 1)
                vec.wait_ge(vec_const, 1)
                vec.wait_ge(const_in, 12 * 16)
                wf32 = dtmp[:, 0:4, :].rearrange("p a b -> p (a b)")
                vec.tensor_copy(bmat[0:1, :], dtmp[0:1, Q, :])
                vec.tensor_copy(bmat[32:33, :], dtmp[32:33, Q, :])
                go(vec.tensor_copy(wfh[:, :], wf32))
                vec.tensor_tensor(wfl[:, :], wf32, f32(wfh[:, :]), ALU.subtract)
                go(vec.tensor_tensor(dtmp[32:33, Q + 1, :], dtmp[32:33, Q, :], f32(bmat[32:33, :]), ALU.subtract))
                go(vec.tensor_copy(bmat[32:33, :], dtmp[32:33, Q + 1, :]))
                vec.wait_ge(kt_in, IR * 16)
                vec.tensor_reduce(kout[:, 0:1], stage_flat, AX.X, ALU.max, apply_absolute_value=True).then_inc(kmax_part, 1)
                vec.wait_ge(kmax_all, 1)
                go(vec.tensor_scalar(kout[:, 3:4], kout[:, 1:2], 1e-30, 1.0 / WSCALE, ALU.max, ALU.mult))
                go(vec.reciprocal(kout[:, 0:1], kout[:, 3:4]))
                go(vec.tensor_scalar(kout[:, 2:3], kout[:, 3:4], 1.0 / XSCALE, None, ALU.mult))
                go(vec.tensor_scalar(kh_flat, stage_flat, kout[:, 0:1], None, ALU.mult))
                vec.scalar_tensor_tensor(out=kl_flat, in0=stage_flat, scalar=kout[:, 0:1], in1=kh_flat,
                                         op0=ALU.mult, op1=ALU.subtract).then_inc(vec_const, 2)

            def inverse_root(out_, sd, half_v, go):
                go(vec.reciprocal(out_, sd))
                go(vec.tensor_tensor(sd, out_, out_, ALU.mult))
                go(vec.tensor_tensor(sd, sd, half_v, ALU.mult))
                return vec.scalar_tensor_tensor(out=out_, in0=sd, scalar=1.5, in1=out_, op0=ALU.add, op1=ALU.mult)

            def prep_piece(n, i, first=False, parts=(0, 1)):
                c, band = divmod(i, BANDS)
                if first:
                    vec.wait_ge(x_in[c], 16)
                    src = xb[:, c, band * BAND:(band + 1) * BAND]
                else:
                    vec.wait_ge(staged[i % STAGES], ((n - 1) * BANDS + i // STAGES + 1) * 16)
                    src = x_stage[:, i % STAGES, :]
                for half in range(2) if 0 in parts else ():
                    vec.bn_stats(bst[:, c, 2 * band + half, :], src[:, half * HALF:(half + 1) * HALF])
                if 1 in parts:
                    vec.tensor_reduce(mx[:, c, 3 * band:3 * band + 3], src.rearrange("p (r l w) -> p l r w", r=CELL, l=3),
                                      AX.XY, ALU.max).then_inc(prep_done, 1)

            PREP_LINKS = 8

            def prep_means(n):
                vec.wait_ge(prep_done, PIECES * (n + 1))
                vec.tensor_copy(cent[:, :, 0:TAPS], mx[:, :, :])
                for c in range(Q):
                    ins = vec.bn_aggr(mv[:, c, :], bst[:, c].rearrange("p t s -> p (t s)"))
                ins.then_inc(stat_ready, 1)

            def prep_variances(n):
                vec.wait_ge(stat_mm, 3 * n + 1)
                vec.tensor_scalar(negm[:, :], ps[:, 0:Q], -1.0, None, ALU.mult).then_inc(negm_done, 1)
                vec.wait_ge(negm_done, n + 1)
                vec.tensor_tensor(va[:, 0, :], mv[:, :, 0], negm[:, :], ALU.add).then_inc(dve_prep, 1)
                vec.wait_ge(dve_prep, PREP_LINKS * n + 1)
                vec.tensor_tensor(va[:, 1, :], va[:, 0, :], va[:, 0, :], ALU.mult).then_inc(dve_prep, 1)
                vec.wait_ge(dve_prep, PREP_LINKS * n + 2)
                vec.tensor_tensor(va[:, 2, :], va[:, 1, :], mv[:, :, 1], ALU.add).then_inc(stat_ready, 1)
                for c in range(Q):
                    vec.tensor_scalar(cent[:, c, 0:TAPS], cent[:, c, 0:TAPS], negm[:, c:c + 1], None, ALU.add)
                vec.tensor_copy(cent[:, :, TAPS], va[:, 0, :]).then_inc(cent_done, 1)

            def prep_scaled(n):
                at = [2]

                def go(ins):
                    at[0] += 1
                    ins.then_inc(dve_prep, 1)
                    vec.wait_ge(dve_prep, PREP_LINKS * n + at[0])
                vec.wait_ge(sd_done, n + 1)
                go(vec.tensor_scalar(va[:, 4, :], ps[:, 8:8 + Q], EPS, -0.5, ALU.add, ALU.mult))
                go(inverse_root(va[:, 5, :], va[:, 3, :], va[:, 4, :], go))
                for c in range(Q):
                    ins = vec.tensor_scalar(wcs[:, c, :], wc[:, c, :], va[:, 5, c:c + 1], None, ALU.mult)
                ins.then_inc(stat_ready, 1)
                vec.wait_ge(stat_ready, 3 * (n + 1))
                go(vec.tensor_copy(wch[:, :, :], wcs[:, :, :]))
                assert at[0] == PREP_LINKS
                vec.tensor_tensor(wcl[:, :, :], wcs[:, :, :], f32(wch[:, :, :]), ALU.subtract).then_inc(wc_done, 1)

            DYN_LINKS = 3

            def dyn_inputs(n):
                vec.wait_ge(stat_mm, 3 * n + 3)
                vec.tensor_scalar(ggs[:, :], ps[:, 16:16 + TAPS + 1], bcc[:, 0:1], 0.0, ALU.add, ALU.max).then_inc(dve_dyn, 1)
                vec.wait_ge(dve_dyn, DYN_LINKS * n + 1)
                vec.scalar_tensor_tensor(out=gk[:, :], in0=kk9[:, 0, :], scalar=ggs[:, TAPS:TAPS + 1], in1=kk9[:, 1, :],
                                         op0=ALU.mult, op1=ALU.add).then_inc(dve_dyn, 1)

            def dyn_maxima(n):
                for k in range(TAPS):
                    ins = vec.scalar_tensor_tensor(out=dtmp[:, k, :], in0=rows[:, 1, :], scalar=ggs[:, k:k + 1], in1=rows[:, 2, :],
                                                   op0=ALU.mult, op1=ALU.add)
                ins.then_inc(dve_dyn, 1)

            def dyn_global(n):
                vec.wait_ge(dve_dyn, DYN_LINKS * n + 3)
                for k in range(TAPS):
                    ins = vec.scalar_tensor_tensor(out=dtmp[:, k, :], in0=rows[:, 0, :], scalar=gk[:, k:k + 1], in1=dtmp[:, k, :],
                                                   op0=ALU.mult, op1=ALU.add)
                ins.then_inc(dyn_sum, 1)

            def dyn_low(n):
                vec.wait_ge(dyn_hi, n + 1)
                vec.scalar_tensor_tensor(out=dynl[:, :, :], in0=dtmp[:, :, :], scalar=0.0, in1=f32(dynh[:, :, :]),
                                         op0=ALU.max, op1=ALU.subtract).then_inc(dyn_done, 1)

            STAT_LINKS = 9
            def x1_means(n):
                vec.wait_ge(x1_done, (n + 1) * X1_OPS)
                vec.tensor_reduce(vb[:, 0, :], sums[:, :, :], AX.X, ALU.add).then_inc(dve_stat, 1)
                vec.wait_ge(dve_stat, STAT_LINKS * n + 1)
                vec.tensor_scalar(nmean[:, :], vb[:, 0, :], -1.0 / PX, None, ALU.mult).then_inc(nmean_done, 1)

            def x1_group_means(n):
                vec.wait_ge(stat_mm2, 2 * n + 1)
                reached(vec, x1_out, n * 80)
                vec.tensor_scalar(mrow[:, :, :], ps[:, 32:32 + Q].unsqueeze(2).to_broadcast([P, Q, W]), -1.0, None,
                                  ALU.mult).then_inc(mrow_done, 1)
                vec.tensor_tensor(vb[:, 1, :], ps[:, 32:32 + Q], nmean[:, :], ALU.subtract).then_inc(dve_stat, 1)
                vec.wait_ge(dve_stat, STAT_LINKS * n + 2)
                vec.tensor_tensor(vb[:, 2, :], vb[:, 1, :], vb[:, 1, :], ALU.mult).then_inc(dve_stat, 1)

            def x1_variances(n):
                vec.wait_ge(sq_done, (n + 1) * Q)
                vec.wait_ge(dve_stat, STAT_LINKS * n + 3)
                vec.scalar_tensor_tensor(out=vb[:, 0, :], in0=m2[:, :], scalar=1.0 / PX, in1=vb[:, 2, :],
                                         op0=ALU.mult, op1=ALU.add).then_inc(dve_stat, 1)
                vec.wait_ge(dve_stat, STAT_LINKS * n + 4)
                mask = ind8[:, :].unsqueeze(1).to_broadcast([P, Q, GQ])
                vec.tensor_tensor(spread[:, 0], nmean[:, :].unsqueeze(2).to_broadcast([P, Q, GQ]), mask, ALU.mult)
                vec.tensor_tensor(spread[:, 1], vb[:, 0, :].unsqueeze(2).to_broadcast([P, Q, GQ]), mask,
                                  ALU.mult).then_inc(stat_ready2, 1)

            def x1_scales(n):
                vec.wait_ge(sd2_done, n + 1)
                vec.tensor_scalar(vt[:, 1, :], ps[:, 96:96 + G], -0.5 * XSCALE ** -2, -0.5 * EPS * XSCALE ** -2, ALU.mult,
                                  ALU.add).then_inc(dve_stat, 1)
                vec.wait_ge(dve_stat, STAT_LINKS * n + 5)
                at = [5]

                def go(ins):
                    at[0] += 1
                    ins.then_inc(dve_stat, 1)
                    vec.wait_ge(dve_stat, STAT_LINKS * n + at[0])
                reached(vec, u_done, n * G)
                go(inverse_root(s_t[:, :], vt[:, 0, :], vt[:, 1, :], go))
                vec.tensor_tensor(b_t[:, :], ps[:, 64:64 + G], s_t[:, :], ALU.mult).then_inc(st_done, 1)
                assert at[0] == STAT_LINKS

            def x_low(n, i):
                t, c = divmod(i, Q)
                r0, nr = TILES[t]
                vec.wait_ge(xs_hi, n * UNITS + i + 1)
                vec.scalar_tensor_tensor(out=xs[:, i % XS_RING, 1, 0:nr * W], in0=xb[:, c, r0 * W:(r0 + nr) * W],
                                         scalar=negm[:, c:c + 1], in1=f32(xs[:, i % XS_RING, 0, 0:nr * W]),
                                         op0=ALU.add, op1=ALU.subtract).then_inc(xs_lo, 1)

            def f_low(n, t):
                r0, nr = TILES[t]
                vec.wait_ge(f_hi, n * NT + t + 1)
                vec.scalar_tensor_tensor(out=fl[:, r0 + 1:r0 + 1 + nr, 1:W + 1],
                                         in0=pac[t % 2][:, 0:nr * W].rearrange("p (r w) -> p r w", w=W), scalar=0.0,
                                         in1=f32(fh[:, r0 + 1:r0 + 1 + nr, 1:W + 1]), op0=ALU.max,
                                         op1=ALU.subtract).then_inc(f_lo, 1)

            def y_low(n, t):
                nr = TILES[t][1]
                vec.wait_ge(y_hi, n * NT + t + 1)
                vec.scalar_tensor_tensor(out=xs[:, t % 2, 1, 0:nr * W], in0=pb[t % 2][:, 0:nr * W], scalar=badc[:, 0:1],
                                         in1=f32(xs[:, t % 2, 0, 0:nr * W]), op0=ALU.add,
                                         op1=ALU.subtract).then_inc(y_lo, 1)

            def residual(n, t, c):
                if t == 0 and c == 0:
                    reached(vec, x1_out, n * 80)
                vec.wait_ge(c_mm, n * UNITS + t * Q + c + 1)
                acc = pac[(t * Q + c) % C_BANKS]
                r0 = TILES[t][0]
                for j, (r, m) in enumerate(PARTS[t]):
                    k, b = r % OR_, r // OR_
                    vec.scalar_tensor_tensor(
                        out=x1b[:, c, k:k + m, b, :], in0=acc[:, (r - r0) * W:(r - r0 + m) * W].rearrange("p (r w) -> p r w", w=W),
                        scalar=bfc[:, c:c + 1], in1=xb[:, c, r * W:(r + m) * W].rearrange("p (r w) -> p r w", w=W),
                        op0=ALU.add, op1=ALU.add,
                        accum_out=sums[:, c, PART_SUM[t] + j:PART_SUM[t] + j + 1]).then_inc(x1_done, 1)

            def output(n, g):
                vec.wait_ge(d_mm, n * G + g + 1)
                dst = t_slot(g // GQ)[0:M6, g % GQ]
                vec.scalar_tensor_tensor(out=dst, in0=pd[g % 2][0:M6, 0:BW].rearrange("p (b w) -> p b w", w=W),
                                         scalar=kout[0:M6, 2:3], in1=dst, op0=ALU.mult, op1=ALU.add).then_inc(out_done, 1)

            def step(n, d=True, more=True):
                for t in range(NT):
                    for c in range(Q):
                        x_low(n, t * Q + c)
                    if t:
                        f_low(n, t - 1)
                    if d and t == 1:
                        x1_scales(n - 1)
                f_low(n, NT - 1)
                dyn_steps = [dyn_inputs, dyn_maxima, dyn_global]
                for g in range(D_FIRST):
                    if d:
                        output(n - 1, g)
                    if dyn_steps:
                        dyn_steps.pop(0)(n)
                    if g == D_FIRST - 2:
                        dyn_low(n)
                    if more and g in PREP_AT:
                        i, part = divmod(PREP_AT.index(g), 2)
                        prep_piece(n + 1, i, parts=(part,))
                for i in PREP_IN_B[0] if more else ():
                    prep_piece(n + 1, i)
                y_low(n, 0)
                for t in range(1, NT):
                    for c in range(Q):
                        residual(n, t - 1, c)
                        if more and c < len(PREP_IN_B[t]):
                            prep_piece(n + 1, PREP_IN_B[t][c])
                    y_low(n, t)
                late = {D_FIRST: (0, 1), D_FIRST + 1: (2, 3)}
                for g in range(D_FIRST, G):
                    for c in late.get(g, ()):
                        residual(n, NT - 1, c)
                    if d:
                        output(n - 1, g)
                    if g == D_FIRST + 1:
                        x1_means(n)
                    if g == AT_MEANS:
                        x1_group_means(n)
                        if more:
                            prep_means(n + 1)
                    if g == AT_SUMS[0] and more:
                        prep_variances(n + 1)
                    if g == AT_SCALED and more:
                        prep_scaled(n + 1)
                    if g == AT_VARIANCES:
                        x1_variances(n)

            constants()
            vec.wait_ge(pool_const, 6)
            for i in range(PIECES):
                prep_piece(0, i, first=True)
            prep_means(0)
            prep_variances(0)
            prep_scaled(0)
            images(vec, step)
            x1_scales(N - 1)
            for g in range(G):
                output(N - 1, g)

        @block.tensor
        def _(pe):
            def three(acc, high_w, low_w, high_x, low_x, start, stop):
                pe.matmul(acc, high_w, high_x, start=start, stop=False)
                pe.matmul(acc, high_w, low_x, start=False, stop=False)
                return pe.matmul(acc, low_w, high_x, start=False, stop=stop)

            def a_tile(n, t):
                nr = TILES[t][1]
                if t >= 2:
                    pe.wait_ge(f_lo, n * NT + t - 1)
                acc = pac[t % 2][:, 0:nr * W]
                pe.matmul(acc.rearrange("p (r w) -> p r w", w=W), bmat[:, :], onesr[:, :].unsqueeze(1).to_broadcast([P, nr, W]),
                          start=True, stop=False)
                for c in range(Q):
                    i = t * Q + c
                    pe.wait_ge(xs_lo, n * UNITS + i + 1)
                    three(acc, wch[:, c, :], wcl[:, c, :], xs[:, i % XS_RING, 0, 0:nr * W], xs[:, i % XS_RING, 1, 0:nr * W],
                          False, c == Q - 1).then_inc(a_mm, 1)

            def c_unit(n, t, c):
                nr = TILES[t][1]
                if c == 0:
                    pe.wait_ge(y_lo, n * NT + t + 1)
                i = t * Q + c
                if i >= C_BANKS:
                    j = i - C_BANKS
                    pe.wait_ge(x1_done, n * X1_OPS + x1_count(j // Q, j % Q))
                three(pac[i % C_BANKS][:, 0:nr * W], wfh[:, c * P:(c + 1) * P], wfl[:, c * P:(c + 1) * P],
                      xs[:, t % 2, 0, 0:nr * W], xs[:, t % 2, 1, 0:nr * W], True, True).then_inc(c_mm, 1)

            def b_tile(n, t):
                r0, nr = TILES[t]
                pe.wait_ge(f_lo, n * NT + min(t + 2, NT))
                reached(pe, y_lo, n * NT + t - 1 if t >= 2 else n * NT)
                acc = pb[t % 2][:, 0:nr * W].rearrange("p (r w) -> p r w", w=W)
                for k in range(TAPS):
                    dy, dx = divmod(k, 3)
                    ins = three(acc, dynh[:, k, :], dynl[:, k, :], fh[:, r0 + dy:r0 + dy + nr, dx:dx + W],
                                fl[:, r0 + dy:r0 + dy + nr, dx:dx + W], k == 0, k == TAPS - 1)
                    if k == TAPS - 1:
                        ins.then_inc(b_mm, 1)
                    if t and k in C_AFTER:
                        c_unit(n, t - 1, C_AFTER.index(k))

            def d_group(n, g):
                pe.wait_ge(hl_lo, n * G + g + 1)
                reached(pe, out_done, n * G + g - 1)
                acc = pd[g % 2][0:M6, 0:BW].rearrange("p (b w) -> p b w", w=W)
                s = g % HL_RING
                for dx in range(3):
                    ins = three(acc, k_h[:, g, dx, :], k_l[:, g, dx, :], hl[:, s, 0, :, dx:dx + W], hl[:, s, 1, :, dx:dx + W],
                                dx == 0, dx == 2)
                ins.then_inc(d_mm, 1)

            def group_mean(n):
                pe.wait_ge(stat_ready, 3 * n + 1)
                pe.matmul(ps[:, 0:Q], ind_m, mv[:, :, 0], start=True, stop=True).then_inc(stat_mm, 1)

            def group_variance(n):
                pe.wait_ge(stat_ready, 3 * n + 2)
                pe.matmul(ps[:, 8:8 + Q], ind_m, va[:, 2, :], start=True, stop=True).then_inc(stat_mm, 1)

            def kernel_inputs(n):
                pe.wait_ge(stat_ready, 3 * n + 3)
                pe.wait_ge(cent_done, n + 1)
                for c in range(Q):
                    ins = pe.matmul(ps[:, 16:16 + TAPS + 1], wcs[:, c, :], cent[:, c, :], start=c == 0, stop=c == Q - 1)
                ins.then_inc(stat_mm, 1)

            def x1_group_means(n):
                pe.wait_ge(nmean_done, n + 1)
                pe.matmul(ps[:, 32:32 + Q], ind_m, nmean[:, :], start=True, stop=True).then_inc(stat_mm2, 1)

            def x1_spread(n):
                pe.wait_ge(stat_ready2, n + 1)
                pe.matmul(ps[:, 64:64 + 2 * G], ones[:, :], spread[:, :, :, :].rearrange("p a q j -> p (a q j)"),
                          start=True, stop=True).then_inc(stat_mm2, 1)

            def step(n, d=True, more=True):
                pe.wait_ge(wc_done, n + 1)
                reached(pe, x1_done, n * X1_OPS)
                for t in range(NT):
                    a_tile(n, t)
                kernel_inputs(n)
                if d:
                    for g in range(D_FIRST):
                        d_group(n - 1, g)
                pe.wait_ge(dyn_done, n + 1)
                for t in range(NT):
                    b_tile(n, t)
                late = {D_FIRST: (0, 1), D_FIRST + 1: (2, 3)}
                for g in range(D_FIRST, G):
                    for c in late.get(g, ()):
                        c_unit(n, NT - 1, c)
                    if d:
                        d_group(n - 1, g)
                    if g == AT_MEANS:
                        x1_group_means(n)
                    if g == AT_SUMS[0] and more:
                        group_mean(n + 1)
                    if g == AT_SUMS[1] and more:
                        group_variance(n + 1)
                    if g == G - 1:
                        x1_spread(n)

            ind_m = ind[:, :, :].rearrange("p j c -> p (j c)")
            pe.wait_ge(pool_const, 6)
            pe.wait_ge(vec_const, 3)
            group_mean(0)
            group_variance(0)
            images(pe, step)
            for g in range(G):
                d_group(N - 1, g)


INPUTS = ["x", "wct", "bc", "wkk", "bkk", "wck", "bck", "b_ad", "wft", "bf", "kt"]


def kernel(x, L0_conv_Wc, L0_conv_bc, L0_conv_Wkk, L0_conv_bkk, L0_conv_Wck, L0_conv_bck, L0_conv_b_ad, L0_conv_Wf,
           L0_conv_bf, L1_conv_kernels):
    import numpy as np
    from concourse import bacc
    from concourse.bass_utils import run_bass_kernel_spmd

    laid_out = {
        "x": np.asarray(x),
        "wct": np.asarray(L0_conv_Wc).reshape(CM, Q, P).transpose(2, 1, 0),
        "bc": np.asarray(L0_conv_bc),
        "wkk": np.asarray(L0_conv_Wkk),
        "bkk": np.asarray(L0_conv_bkk),
        "wck": np.asarray(L0_conv_Wck).T,
        "bck": np.asarray(L0_conv_bck),
        "b_ad": np.asarray(L0_conv_b_ad),
        "wft": np.asarray(L0_conv_Wf).T,
        "bf": np.asarray(L0_conv_bf).reshape(Q, P).T,
        "kt": np.asarray(L1_conv_kernels).reshape(G, GC, GC, 3, 3).transpose(2, 0, 4, 3, 1)[:, :, :, ::-1, :].reshape(GC, G * 3, 3 * GC),
    }
    nc = bacc.Bacc("TRN2", target_bir_lowering=False, num_devices=1, dynamic_dma_scratch_size=1024)
    arrays, aps = {}, {}
    for name in INPUTS:
        a = np.ascontiguousarray(laid_out[name])
        arrays[name] = a
        aps[name] = nc.dram_tensor(name, a.shape, mybir.dt.from_np(a.dtype), kind="ExternalInput").ap()
    out = nc.dram_tensor("out", (N, Q, M6, GQ * BW), F32, kind="ExternalOutput").ap()
    build(nc, *[aps[name] for name in INPUTS], out)
    r = run_bass_kernel_spmd(nc, [arrays], core_ids=[0])
    got = r.results[0]["out"].reshape(N, Q, OR_, GC, GQ, NB, W)
    return np.ascontiguousarray(got.transpose(0, 1, 4, 3, 5, 2, 6)).reshape(N, C, H, W)
```

```python
from contextlib import ExitStack

import concourse.bass as bass
from concourse import mybir

F32 = mybir.dt.float32
F32R = mybir.dt.float32r
F16 = mybir.dt.float16
ALU = mybir.AluOpType
ACT = mybir.ActivationFunctionType
AX = mybir.AxisListType

P = 128
N, C, H, W = 32, 512, 48, 48
Q = C // P
PX = H * W
CM = 128
TAPS = 9
GC = 16
GQ = P // GC
G = C // GC
OR_ = 6
IR = OR_ + 2
NB = H // OR_
M6 = OR_ * GC
BW = NB * W
SLOTS = H + 2
TILES = [(0, 10), (10, 10), (20, 10), (30, 10), (40, 8)]
NT = len(TILES)
X_TILES = ((0, 3), (3, NT))
MAXW = 480
UNITS = NT * Q
EPS = 1e-5
XSCALE = 256.0
WSCALE = 8192.0

XS_RING, HL_RING, U_RING = 5, 4, 2
C_BANKS = 3
C_AFTER = (2, 4, 6, 8)
D_FIRST = 13
EARLY = 3
LATE = {D_FIRST + 1: (0, 1), D_FIRST + 2: (2, 3)}
AT_X1_SUMS = D_FIRST + 2
AT_X1_MEANS = D_FIRST + 3
AT_SQUARES = (18, 20, 23, 26)
AT_X1_VARIANCES = 30
AT_MEANS = D_FIRST + 4
AT_SUMS = (D_FIRST + 5, D_FIRST + 7)
AT_VARIANCES = D_FIRST + 6
AT_ROOT = D_FIRST + 9
AT_SCALED = D_FIRST + 9
AT_X_LOW = (28, 29, 30, 31)
AT_SCALES = 6
SQ_BLOCKS = ((0, 3), (3, 5), (5, 8))
SQUARES = Q * len(SQ_BLOCKS)
PREP_AT = (5, 6, 7, 8, 9, 11)
PREP_IN_B = (4, 2)
DYN_LOW_AT = 10
CELL = 16
BANDS = H // CELL
BAND = CELL * W
PIECES = Q * BANDS
assert 2 * PIECES == len(PREP_AT) + sum(PREP_IN_B) + (NT - 1) * (Q - 1)
STAGES = 4
HALF = BAND // 2


def row_parts(r0, rows):
    out, r = [], r0
    while r < r0 + rows:
        e = min(r0 + rows, (r // OR_ + 1) * OR_)
        out.append((r, e - r))
        r = e
    return out


PARTS = [row_parts(r0, rows) for r0, rows in TILES]
PART_SUM = [sum(len(p) for p in PARTS[:t]) for t in range(NT + 1)]
X1_OPS = Q * PART_SUM[NT]


def x1_count(t, c):
    return Q * PART_SUM[t] + (c + 1) * len(PARTS[t])


def partition_of(p):
    return GC * {0: 6, 7: 7}.get(p, p - 1)


T_SLOT = [0, 1, 0, 2]


def build(nc, x, wct, bc, wkk, bkk, wck, bck, b_ad, wft, bf, kt, out):
    x_d = x.rearrange("n (q p) h w -> n p q (h w)", q=Q)
    scratch = nc.dram_tensor("x1_rows", (N, C, SLOTS, W), F32, kind="Internal").ap()
    sc_w = scratch.rearrange("n (q p) s w -> n p q (s w)", q=Q)
    sc_r = scratch.rearrange("n (q j c) s w -> n q c j (s w)", q=Q, c=GC)

    with ExitStack() as ctx:
        def sb(name, shape, dt=F32):
            return ctx.enter_context(nc.sbuf_tensor(name, shape, dt))

        def bank(name):
            return ctx.enter_context(nc.psum_tensor(name, [P, 512], F32))

        def sem(name):
            return ctx.enter_context(nc.semaphore(name))

        xb = sb("xb", [P, Q, PX])
        x1b = sb("x1b", [P, Q, OR_, NB, W])
        mrow = sb("mrow", [P, Q, W])
        tb = sb("tb", [P, 3, GQ, NB, W])
        fh = sb("fh", [P, H + 2, W + 2], F32R)
        fl = sb("fl", [P, H + 2, W + 2], F32R)
        k_h = sb("k_h", [P, G, 3, M6], F16)
        k_l = sb("k_l", [P, G, 3, M6], F16)
        xs = sb("xs", [P, XS_RING, 2, MAXW], F32R)
        hl = sb("hl", [P, HL_RING, 2, NB, W + 2], F16)
        un = sb("un", [P, U_RING, NB, W])
        dynh = sb("dynh", [P, TAPS, CM], F32R)
        dynl = sb("dynl", [P, TAPS, CM], F32R)
        dtmp = sb("dtmp", [P, TAPS, CM])
        wc = sb("wc", [P, Q, CM])
        wch = sb("wch", [P, Q, CM], F32R)
        wcl = sb("wcl", [P, Q, CM], F32R)
        wfh = sb("wfh", [P, C], F32R)
        wfl = sb("wfl", [P, C], F32R)
        rows = sb("rows", [P, 3, CM])
        ind = sb("ind", [P, GQ, GC])
        ones = sb("ones", [P, P])
        bmat = sb("bmat", [P, CM], F32R)
        onesr = sb("onesr", [P, W], F32R)
        ind8 = sb("ind8", [P, GQ])
        bcc = sb("bcc", [P, 1])
        badc = sb("badc", [P, 1])
        bfc = sb("bfc", [P, Q])
        kk9 = sb("kk9", [P, 2, TAPS])
        eps = sb("eps", [P, 2])
        kout = sb("kout", [P, 4])
        bst = sb("bst", [P, Q, 2 * BANDS, 6])
        mv = sb("mv", [P, Q, 2])
        cent = sb("cent", [P, Q, TAPS + 1])
        mx = sb("mx", [P, Q, TAPS])
        negm = sb("negm", [P, Q])
        va = sb("va", [P, 6, Q])
        ggs = sb("ggs", [P, TAPS + 1])
        gk = sb("gk", [P, TAPS])
        sums = sb("sums", [P, Q, PART_SUM[NT]])
        nmean = sb("nmean", [P, Q])
        cen = sb("cen", [P, Q])
        m2 = sb("m2", [P, Q, len(SQ_BLOCKS)])
        vb = sb("vb", [P, 5, Q])
        spread = sb("spread", [P, 2, Q, GQ])
        vt = sb("vt", [P, 5, G])
        s_t = sb("s_t", [P, G])
        b_t = sb("b_t", [P, G])

        pac = [bank(f"pac{i}") for i in range(C_BANKS)]
        pb = [bank(f"pb{i}") for i in range(2)]
        pd = [bank(f"pd{i}") for i in range(2)]
        ps = bank("ps")

        const_in = sem("const_in")
        kt_in = sem("kt_in")
        x_first = [sem(f"x_first{c}") for c in range(Q)]
        x_in = [sem(f"x_in{i}") for i in range(2)]
        t_in = [sem(f"t_in{c}") for c in range(Q)]
        staged = [sem(f"staged{i}") for i in range(STAGES)]
        x1_out = sem("x1_out")
        stored = [sem(f"stored{c}") for c in range(Q)]
        pool_const = sem("pool_const")
        kmax_all = sem("kmax_all")
        kmax_part = sem("kmax_part")
        vec_const = sem("vec_const")
        dve_const = sem("dve_const")
        dve_prep = sem("dve_prep")
        dve_dyn = sem("dve_dyn")
        dve_stat = sem("dve_stat")
        prep_done = sem("prep_done")
        stat_ready = sem("stat_ready")
        cent_done = sem("cent_done")
        dyn_sum = sem("dyn_sum")
        dyn_hi = sem("dyn_hi")
        stat_mm = sem("stat_mm")
        stat_mm2 = sem("stat_mm2")
        stat_ready2 = sem("stat_ready2")
        sd_done = sem("sd_done")
        sd2_done = sem("sd2_done")
        negm_done = sem("negm_done")
        wc_done = sem("wc_done")
        dyn_done = sem("dyn_done")
        st_done = sem("st_done")
        mrow_done = sem("mrow_done")
        nmean_done = sem("nmean_done")
        xs_hi = sem("xs_hi")
        xs_lo = sem("xs_lo")
        a_mm = sem("a_mm")
        f_hi = sem("f_hi")
        f_lo = sem("f_lo")
        b_mm = sem("b_mm")
        y_hi = sem("y_hi")
        y_lo = sem("y_lo")
        c_mm = sem("c_mm")
        x1_done = sem("x1_done")
        cen_done = sem("cen_done")
        sq_done = sem("sq_done")
        var_done = sem("var_done")
        u_done = sem("u_done")
        hl_hi = sem("hl_hi")
        hl_lo = sem("hl_lo")
        d_mm = sem("d_mm")
        out_done = sem("out_done")

        def f32(ap):
            return ap.bitcast(F32)

        wcs = dtmp[:, 0:Q, :]
        stage = tb[:, :, :, :, :].rearrange("p a j b w -> p (a j b w)").rearrange("p (g m) -> p g m", m=M6)
        stage_flat = tb[:, :, :, :, :].rearrange("p a j b w -> p (a j b w)")
        kh_flat = k_h[:, :, :, :].rearrange("p g t m -> p (g t m)")
        kl_flat = k_l[:, :, :, :].rearrange("p g t m -> p (g t m)")

        x_stage = stage_flat[:, 2 * GQ * BW:].rearrange("p (s m) -> p s m", s=STAGES)

        def t_slot(c):
            return tb[:, T_SLOT[c], :, :, :]

        def reached(eng, semaphore, value):
            if not isinstance(value, int) or value > 0:
                eng.wait_ge(semaphore, value)

        def images(eng, step):
            step(0, d=False)
            step(1)
            with eng.Fori(2, N - 1) as n:
                step(n)
            step(N - 1, more=False)

        block = ctx.enter_context(nc.Block())

        @block.sync
        def _(sp):
            def load_x(n, part):
                t0, t1 = X_TILES[part]
                sp.wait_ge(x1_done, (n - 1) * X1_OPS + Q * PART_SUM[t1])
                lo, hi = TILES[t0][0] * W, (TILES[t1 - 1][0] + TILES[t1 - 1][1]) * W
                sp.dma_start(xb[:, :, lo:hi], x_d[n, :, :, lo:hi]).then_inc(x_in[part], 16)

            def stage_x(n, pieces):
                for i in pieces:
                    c, band = divmod(i, BANDS)
                    sp.wait_ge(prep_done, PIECES * n + i - STAGES + 1 if i >= STAGES else PIECES * n)
                    sp.dma_start(x_stage[:, i % STAGES, :], x_d[n, :, c, band * BAND:(band + 1) * BAND]).then_inc(staged[i % STAGES], 16)

            def write_x1(n):
                sp.wait_ge(x1_done, (n + 1) * X1_OPS)
                sp.wait_ge(mrow_done, n + 1)
                dst = sc_w[n]
                src = x1b[:, :, :, :, :].rearrange("p q k b w -> p q (k b w)")
                sp.dma_start(dst[:, :, 0:BW], src[:, :, 0:BW]).then_inc(x1_out, 16)
                sp.dma_start(dst[:, :, BW:BW + W], mrow[:, :, :]).then_inc(x1_out, 16)
                sp.dma_start(dst[:, :, BW + W:5 * BW + W], src[:, :, BW:5 * BW]).then_inc(x1_out, 16)
                sp.dma_start(dst[:, :, 5 * BW + W:5 * BW + 2 * W], mrow[:, :, :]).then_inc(x1_out, 16)
                sp.dma_start(dst[:, :, 5 * BW + 2 * W:], src[:, :, 5 * BW:]).then_inc(x1_out, 16)

            def load_t(n, c):
                if c == 0:
                    sp.wait_ge(x1_out, (n + 1) * 80)
                reached(sp, stored[{0: 2, 2: 0}.get(c, c)], (n + 1 if c == 2 else n) * 16)
                for p in range(IR):
                    at = {0: 5 * BW + W, 1: 0, 6: 5 * BW + 2 * W, 7: W}.get(p, (p - 1) * BW + W)
                    k = partition_of(p)
                    sp.dma_start(t_slot(c)[k:k + GC].rearrange("c j b w -> c j (b w)"),
                                 sc_r[n, c, :, :, at:at + BW]).then_inc(t_in[c], 16)

            def store(n, c):
                sp.wait_ge(out_done, n * G + (c + 1) * GQ)
                sp.dma_start(out[n, c], t_slot(c)[0:M6].rearrange("p j b w -> p (j b w)")).then_inc(stored[c], 16)

            def step(n, d=True, more=True):
                if more:
                    reached(sp, stored[3], (n - 1) * 16 if d else 0)
                    stage_x(n + 1, range(STAGES + 2))
                if d:
                    store(n - 1, 0)
                    load_t(n - 1, 2)
                if more:
                    stage_x(n + 1, range(STAGES + 2, PIECES))
                    load_x(n + 1, 0)
                    sp.wait_ge(prep_done, PIECES * (n + 2))
                if d:
                    load_t(n - 1, 3)
                if more:
                    load_x(n + 1, 1)
                write_x1(n)
                if d:
                    store(n - 1, 1)
                    store(n - 1, 2)
                load_t(n, 0)
                load_t(n, 1)
                if d:
                    store(n - 1, 3)

            for c in range(Q):
                sp.dma_start(xb[:, c, :], x_d[0, :, c, :]).then_inc(x_first[c], 16)
            for dst, src in ((wc[:, :, :], wct), (dtmp[:, 0:4, :].rearrange("p a b -> p (a b)"), wft),
                             (rows[:, 0, :], wck[0].partition_broadcast(P)), (rows[:, 1, :], wck[1].partition_broadcast(P)),
                             (rows[:, 2, :], bck.partition_broadcast(P)), (kk9[:, 0, :], wkk.partition_broadcast(P)),
                             (kk9[:, 1, :], bkk.partition_broadcast(P)), (bcc[:, :], bc.rearrange("(p a) -> p a", a=1)),
                             (badc[:, :], b_ad.rearrange("(p a) -> p a", a=1)), (bfc[:, :], bf),
                             (dtmp[0:1, Q, :], bc.rearrange("(a p) -> a p", a=1)),
                             (dtmp[32:33, Q, :], bc.rearrange("(a p) -> a p", a=1))):
                sp.dma_start(dst, src).then_inc(const_in, 16)
            sp.wait_ge(vec_const, 1)
            for p in range(IR):
                lo, hi = max(0, p - 2), min(OR_ - 1, p)
                k, at = partition_of(p), 2 - p + lo
                sp.dma_start(stage[k:k + GC, :, lo * GC:(hi + 1) * GC],
                             kt[:, :, at * GC:(at + hi - lo + 1) * GC]).then_inc(kt_in, 16)
            sp.wait_ge(vec_const, 3)
            images(sp, step)
            load_t(N - 1, 3)
            store(N - 1, 0)
            load_t(N - 1, 2)
            store(N - 1, 1)
            store(N - 1, 2)
            store(N - 1, 3)
            for c in range(Q):
                sp.wait_ge(stored[c], N * 16)

        @block.gpsimd
        def _(pool):
            pool.memset(ind[:, :, :], 1.0 / GC).then_inc(pool_const, 1)
            pool.memset(ind8[:, :], 1.0).then_inc(pool_const, 1)
            pool.wait_ge(pool_const, 2)
            for n, (base, mult, step_) in enumerate(((0, 1, -GC), (GC - 1, -1, GC))):
                pool.affine_select(out=ind[:, :, :], in_=ind[:, :, :], compare_op=ALU.is_ge, fill=0.0, base=base,
                                   pattern=[[step_, GQ], [0, GC]], channel_multiplier=mult).then_inc(pool_const, 1)
                pool.affine_select(out=ind8[:, :], in_=ind8[:, :], compare_op=ALU.is_ge, fill=0.0, base=base,
                                   pattern=[[step_, GQ]], channel_multiplier=mult).then_inc(pool_const, 1)
                pool.wait_ge(pool_const, 4 + 2 * n)
            pool.wait_ge(kmax_part, 1)
            pool.partition_all_reduce(kout[:, 1:2], kout[:, 0:1], P, bass.bass_isa.ReduceOp.max).then_inc(kmax_all, 1)

            def d_groups(n, groups):
                for g in groups:
                    pool.wait_ge(hl_hi, n * G + g + 1)
                    pool.tensor_tensor(hl[:, g % HL_RING, 1, :, 1:W + 1], un[:, g % U_RING], hl[:, g % HL_RING, 0, :, 1:W + 1],
                                       ALU.subtract).then_inc(hl_lo, 1)

            def step(n, d=True, more=True):
                if d:
                    d_groups(n - 1, range(G))

            images(pool, step)
            d_groups(N - 1, range(G))

        @block.scalar
        def _(act):
            def d_groups(n, groups):
                for g in groups:
                    if g % GQ == 0:
                        act.wait_ge(t_in[g // GQ], (n + 1) * 16 * IR)
                    if g == 0:
                        act.wait_ge(st_done, n + 1)
                    reached(act, hl_lo, n * G + g - U_RING + 1)
                    act.activation(un[:, g % U_RING], t_slot(g // GQ)[:, g % GQ], ACT.Identity,
                                   bias=b_t[:, g:g + 1], scale=s_t[:, g:g + 1]).then_inc(u_done, 1)
                    act.wait_ge(u_done, n * G + g + 1)
                    reached(act, d_mm, n * G + g - HL_RING + 1)
                    act.activation(hl[:, g % HL_RING, 0, :, 1:W + 1], un[:, g % U_RING], ACT.Copy).then_inc(hl_hi, 1)

            def f_high(n, t):
                r0, nr = TILES[t]
                act.wait_ge(a_mm, n * UNITS + Q * (t + 1))
                if t == 0:
                    reached(act, b_mm, n * NT)
                act.activation(fh[:, r0 + 1:r0 + 1 + nr, 1:W + 1], pac[t % 2][:, 0:nr * W].rearrange("p (r w) -> p r w", w=W),
                               ACT.Relu).then_inc(f_hi, 1)

            def a_phase(n, d):
                for t, (r0, nr) in enumerate(TILES):
                    for c in range(Q):
                        i = t * Q + c
                        if i == 0:
                            act.wait_ge(negm_done, n + 1)
                            reached(act, sq_done, n * SQUARES)
                        if not d and t == 0:
                            act.wait_ge(x_first[c], 16)
                        for part, (t0, _) in enumerate(X_TILES):
                            if d and c == 0 and t == t0:
                                act.wait_ge(x_in[part], n * 16)
                        reached(act, a_mm, n * UNITS + i - XS_RING + 1)
                        act.activation(xs[:, i % XS_RING, 0, 0:nr * W], xb[:, c, r0 * W:(r0 + nr) * W], ACT.Identity,
                                       bias=negm[:, c:c + 1]).then_inc(xs_hi, 1)
                    if t:
                        f_high(n, t - 1)
                    if d and t == 1:
                        root_second(n - 1)
                if d:
                    d_groups(n - 1, range(EARLY))
                f_high(n, NT - 1)

            def y_high(n, t):
                nr = TILES[t][1]
                act.wait_ge(b_mm, n * NT + t + 1)
                reached(act, c_mm, n * UNITS + Q * (t - 1) if t >= 2 else n * UNITS)
                act.activation(xs[:, t % 2, 0, 0:nr * W], pb[t % 2][:, 0:nr * W], ACT.Identity,
                               bias=badc[:, 0:1]).then_inc(y_hi, 1)

            def center(n):
                act.wait_ge(x1_done, n * X1_OPS + Q * PART_SUM[1])
                reached(act, var_done, n)
                act.activation(cen[:, :], sums[:, :, 0], ACT.Copy, scale=-1.0 / (OR_ * W)).then_inc(cen_done, 1)

            def square(n, i):
                part, c = divmod(i, Q)
                lo, hi = SQ_BLOCKS[part]
                if i == 0:
                    act.wait_ge(cen_done, n + 1)
                last = (hi * OR_ - 1) // TILES[0][1]
                act.wait_ge(x1_done, n * X1_OPS + x1_count(last, c))
                reached(act, sq_done, n * SQUARES + i)
                m = (hi - lo) * W
                act.activation(xs[:, 2:XS_RING].rearrange("p a b m -> p (a b m)")[:, 0:OR_ * m].rearrange("p (k m) -> p k m", k=OR_),
                               x1b[:, c, :, lo:hi, :].rearrange("p k b w -> p k (b w)"), ACT.Square, bias=cen[:, c:c + 1],
                               accum_out=m2[:, c, part:part + 1]).then_inc(sq_done, 1)

            def root_first(n):
                act.wait_ge(stat_mm, 3 * n + 2)
                act.activation(va[:, 3, :], ps[:, 8:8 + Q], ACT.Sqrt, bias=eps[:, 0:1]).then_inc(sd_done, 1)

            def root_second(n):
                act.wait_ge(stat_mm2, 2 * n + 2)
                act.activation(vt[:, 0, :], ps[:, 96:96 + G], ACT.Sqrt, bias=eps[:, 1:2],
                               scale=XSCALE ** -2).then_inc(sd2_done, 1)

            def step(n, d=True, more=True):
                a_phase(n, d)
                if d:
                    d_groups(n - 1, range(EARLY, D_FIRST))
                act.wait_ge(dyn_sum, 2 * (n + 1))
                act.activation(dynh[:, :, :], dtmp[:, :, :], ACT.Relu).then_inc(dyn_hi, 1)
                for t in range(NT - 1):
                    y_high(n, t)
                    if t == 1:
                        center(n)
                    for c in range(Q) if t >= 2 else ():
                        square(n, (t - 2) * Q + c)
                if d:
                    d_groups(n - 1, range(D_FIRST, D_FIRST + EARLY))
                y_high(n, NT - 1)
                if d:
                    for g in range(D_FIRST + EARLY, G):
                        d_groups(n - 1, [g])
                        if g == AT_ROOT and more:
                            root_first(n + 1)
                        if g in AT_SQUARES:
                            square(n, 2 * Q + AT_SQUARES.index(g))
                else:
                    root_first(n + 1)
                    for c in range(Q):
                        square(n, 2 * Q + c)

            act.wait_ge(vec_const, 3)
            root_first(0)
            images(act, step)
            root_second(N - 1)
            d_groups(N - 1, range(G))

        @block.vector
        def _(vec):
            def chain(semaphore, n, per_image):
                count = [0]

                def go(ins):
                    count[0] += 1
                    assert count[0] <= per_image
                    ins.then_inc(semaphore, 1)
                    vec.wait_ge(semaphore, n * per_image + count[0])
                return go

            def constants():
                go = chain(dve_const, 0, 8)
                vec.memset(f32(fh[:, :, :]), 0.0)
                vec.memset(f32(fl[:, :, :]), 0.0)
                vec.memset(hl[:, :, :, :, :], 0.0)
                vec.memset(f32(onesr[:, :]), 1.0)
                vec.memset(ones[:, :], 1.0 / GC)
                vec.memset(f32(bmat[:, :]), 0.0)
                vec.memset(eps[:, 0:1], EPS)
                vec.memset(eps[:, 1:2], EPS / XSCALE ** 2)
                vec.memset(stage, 0.0).then_inc(vec_const, 1)
                vec.wait_ge(vec_const, 1)
                vec.wait_ge(const_in, 12 * 16)
                wf32 = dtmp[:, 0:4, :].rearrange("p a b -> p (a b)")
                vec.tensor_copy(bmat[0:1, :], dtmp[0:1, Q, :])
                vec.tensor_copy(bmat[32:33, :], dtmp[32:33, Q, :])
                go(vec.tensor_copy(wfh[:, :], wf32))
                vec.tensor_tensor(wfl[:, :], wf32, f32(wfh[:, :]), ALU.subtract)
                go(vec.tensor_tensor(dtmp[32:33, Q + 1, :], dtmp[32:33, Q, :], f32(bmat[32:33, :]), ALU.subtract))
                go(vec.tensor_copy(bmat[32:33, :], dtmp[32:33, Q + 1, :]))
                vec.wait_ge(kt_in, IR * 16)
                vec.tensor_reduce(kout[:, 0:1], stage_flat, AX.X, ALU.max, apply_absolute_value=True).then_inc(kmax_part, 1)
                vec.wait_ge(kmax_all, 1)
                go(vec.tensor_scalar(kout[:, 3:4], kout[:, 1:2], 1e-30, 1.0 / WSCALE, ALU.max, ALU.mult))
                go(vec.reciprocal(kout[:, 0:1], kout[:, 3:4]))
                go(vec.tensor_scalar(kout[:, 2:3], kout[:, 3:4], 1.0 / XSCALE, None, ALU.mult))
                go(vec.tensor_scalar(kh_flat, stage_flat, kout[:, 0:1], None, ALU.mult))
                vec.scalar_tensor_tensor(out=kl_flat, in0=stage_flat, scalar=kout[:, 0:1], in1=kh_flat,
                                         op0=ALU.mult, op1=ALU.subtract).then_inc(vec_const, 2)

            def inverse_root(out_, sd, half_v, go):
                go(vec.reciprocal(out_, sd))
                go(vec.tensor_tensor(sd, out_, out_, ALU.mult))
                go(vec.tensor_tensor(sd, sd, half_v, ALU.mult))
                return vec.scalar_tensor_tensor(out=out_, in0=sd, scalar=1.5, in1=out_, op0=ALU.add, op1=ALU.mult)

            def prep_half(n, h, first=False):
                i, part = divmod(h, 2)
                c, band = divmod(i, BANDS)
                if first:
                    vec.wait_ge(x_first[c], 16)
                    src = xb[:, c, band * BAND:(band + 1) * BAND]
                else:
                    vec.wait_ge(staged[i % STAGES], ((n - 1) * BANDS + i // STAGES + 1) * 16)
                    src = x_stage[:, i % STAGES, :]
                for half in range(2) if part == 0 else ():
                    vec.bn_stats(bst[:, c, 2 * band + half, :], src[:, half * HALF:(half + 1) * HALF])
                if part == 1:
                    vec.tensor_reduce(mx[:, c, 3 * band:3 * band + 3], src.rearrange("p (r l w) -> p l r w", r=CELL, l=3),
                                      AX.XY, ALU.max).then_inc(prep_done, 1)

            PREP_LINKS = 8

            def prep_means(n):
                vec.wait_ge(prep_done, PIECES * (n + 1))
                vec.tensor_copy(cent[:, :, 0:TAPS], mx[:, :, :])
                for c in range(Q):
                    ins = vec.bn_aggr(mv[:, c, :], bst[:, c].rearrange("p t s -> p (t s)"))
                ins.then_inc(stat_ready, 1)

            def prep_variances(n):
                vec.wait_ge(stat_mm, 3 * n + 1)
                vec.tensor_scalar(negm[:, :], ps[:, 0:Q], -1.0, None, ALU.mult).then_inc(negm_done, 1)
                vec.wait_ge(negm_done, n + 1)
                vec.tensor_tensor(va[:, 0, :], mv[:, :, 0], negm[:, :], ALU.add).then_inc(dve_prep, 1)
                vec.wait_ge(dve_prep, PREP_LINKS * n + 1)
                vec.tensor_tensor(va[:, 1, :], va[:, 0, :], va[:, 0, :], ALU.mult).then_inc(dve_prep, 1)
                vec.wait_ge(dve_prep, PREP_LINKS * n + 2)
                vec.tensor_tensor(va[:, 2, :], va[:, 1, :], mv[:, :, 1], ALU.add).then_inc(stat_ready, 1)
                for c in range(Q):
                    vec.tensor_scalar(cent[:, c, 0:TAPS], cent[:, c, 0:TAPS], negm[:, c:c + 1], None, ALU.add)
                vec.tensor_copy(cent[:, :, TAPS], va[:, 0, :]).then_inc(cent_done, 1)

            def prep_scaled(n, step):
                if step == 0:
                    at = [2]

                    def go(ins):
                        at[0] += 1
                        ins.then_inc(dve_prep, 1)
                        vec.wait_ge(dve_prep, PREP_LINKS * n + at[0])
                    vec.wait_ge(sd_done, n + 1)
                    go(vec.tensor_scalar(va[:, 4, :], ps[:, 8:8 + Q], EPS, -0.5, ALU.add, ALU.mult))
                    inverse_root(va[:, 5, :], va[:, 3, :], va[:, 4, :], go).then_inc(dve_prep, 1)
                    assert at[0] == 6
                elif step == 1:
                    vec.wait_ge(dve_prep, PREP_LINKS * n + 7)
                    for c in range(Q):
                        ins = vec.tensor_scalar(wcs[:, c, :], wc[:, c, :], va[:, 5, c:c + 1], None, ALU.mult)
                    ins.then_inc(stat_ready, 1)
                else:
                    vec.wait_ge(stat_ready, 3 * (n + 1))
                    vec.tensor_copy(wch[:, :, :], wcs[:, :, :]).then_inc(dve_prep, 1)
                    vec.wait_ge(dve_prep, PREP_LINKS * (n + 1))
                    vec.tensor_tensor(wcl[:, :, :], wcs[:, :, :], f32(wch[:, :, :]), ALU.subtract).then_inc(wc_done, 1)

            DYN_LINKS = 4
            DYN_HALVES = (range(5, TAPS), range(5))

            def dyn_inputs(n, taps):
                vec.wait_ge(stat_mm, 3 * n + 3)
                vec.tensor_scalar(ggs[:, :], ps[:, 16:16 + TAPS + 1], bcc[:, 0:1], 0.0, ALU.add, ALU.max).then_inc(dve_dyn, 1)
                vec.wait_ge(dve_dyn, DYN_LINKS * n + 1)
                vec.scalar_tensor_tensor(out=gk[:, :], in0=kk9[:, 0, :], scalar=ggs[:, TAPS:TAPS + 1], in1=kk9[:, 1, :],
                                         op0=ALU.mult, op1=ALU.add).then_inc(dve_dyn, 1)

            def dyn_maxima(n, taps):
                for k in taps:
                    ins = vec.scalar_tensor_tensor(out=dtmp[:, k, :], in0=rows[:, 1, :], scalar=ggs[:, k:k + 1], in1=rows[:, 2, :],
                                                   op0=ALU.mult, op1=ALU.add)
                ins.then_inc(dve_dyn, 1)

            def dyn_global(n, taps):
                vec.wait_ge(dve_dyn, DYN_LINKS * (n + 1))
                for k in taps:
                    ins = vec.scalar_tensor_tensor(out=dtmp[:, k, :], in0=rows[:, 0, :], scalar=gk[:, k:k + 1], in1=dtmp[:, k, :],
                                                   op0=ALU.mult, op1=ALU.add)
                ins.then_inc(dyn_sum, 1)

            def dyn_low(n):
                vec.wait_ge(dyn_hi, n + 1)
                vec.scalar_tensor_tensor(out=dynl[:, :, :], in0=dtmp[:, :, :], scalar=0.0, in1=f32(dynh[:, :, :]),
                                         op0=ALU.max, op1=ALU.subtract).then_inc(dyn_done, 1)

            STAT_LINKS = 12
            def x1_means(n):
                vec.wait_ge(x1_done, (n + 1) * X1_OPS)
                vec.tensor_reduce(vb[:, 0, :], sums[:, :, :], AX.X, ALU.add).then_inc(dve_stat, 1)
                vec.wait_ge(dve_stat, STAT_LINKS * n + 1)
                vec.tensor_scalar(nmean[:, :], vb[:, 0, :], -1.0 / PX, None, ALU.mult).then_inc(nmean_done, 1)

            def x1_group_means(n):
                vec.wait_ge(stat_mm2, 2 * n + 1)
                reached(vec, x1_out, n * 80)
                vec.tensor_scalar(mrow[:, :, :], ps[:, 32:32 + Q].unsqueeze(2).to_broadcast([P, Q, W]), -1.0, None,
                                  ALU.mult).then_inc(mrow_done, 1)
                vec.tensor_tensor(vb[:, 1, :], ps[:, 32:32 + Q], nmean[:, :], ALU.subtract).then_inc(dve_stat, 1)
                vec.wait_ge(dve_stat, STAT_LINKS * n + 2)
                vec.tensor_tensor(vb[:, 2, :], vb[:, 1, :], vb[:, 1, :], ALU.mult).then_inc(dve_stat, 1)
                vec.tensor_tensor(vb[:, 3, :], cen[:, :], nmean[:, :], ALU.subtract).then_inc(dve_stat, 1)
                vec.wait_ge(dve_stat, STAT_LINKS * n + 4)
                vec.tensor_tensor(vb[:, 3, :], vb[:, 3, :], vb[:, 3, :], ALU.mult).then_inc(dve_stat, 1)
                vec.wait_ge(dve_stat, STAT_LINKS * n + 5)
                vec.tensor_tensor(vb[:, 2, :], vb[:, 2, :], vb[:, 3, :], ALU.subtract).then_inc(dve_stat, 1)

            def x1_variances(n):
                vec.wait_ge(sq_done, (n + 1) * SQUARES)
                vec.tensor_reduce(vb[:, 4, :], m2[:, :, :], AX.X, ALU.add).then_inc(dve_stat, 1)
                vec.wait_ge(dve_stat, STAT_LINKS * n + 7)
                vec.scalar_tensor_tensor(out=vb[:, 0, :], in0=vb[:, 4, :], scalar=1.0 / PX, in1=vb[:, 2, :],
                                         op0=ALU.mult, op1=ALU.add).then_inc(var_done, 1)
                vec.wait_ge(var_done, n + 1)
                mask = ind8[:, :].unsqueeze(1).to_broadcast([P, Q, GQ])
                vec.tensor_tensor(spread[:, 0], nmean[:, :].unsqueeze(2).to_broadcast([P, Q, GQ]), mask, ALU.mult)
                vec.tensor_tensor(spread[:, 1], vb[:, 0, :].unsqueeze(2).to_broadcast([P, Q, GQ]), mask,
                                  ALU.mult).then_inc(stat_ready2, 1)

            SCALE_STEPS = 6

            def x1_scales(n, step):
                if step:
                    vec.wait_ge(dve_stat, STAT_LINKS * n + 7 + step)
                if step == 0:
                    vec.wait_ge(sd2_done, n + 1)
                    vec.tensor_scalar(vt[:, 1, :], ps[:, 96:96 + G], -0.5 * XSCALE ** -2, -0.5 * EPS * XSCALE ** -2, ALU.mult,
                                      ALU.add).then_inc(dve_stat, 1)
                elif step == 1:
                    reached(vec, u_done, n * G)
                    vec.reciprocal(s_t[:, :], vt[:, 0, :]).then_inc(dve_stat, 1)
                elif step == 2:
                    vec.tensor_tensor(vt[:, 0, :], s_t[:, :], s_t[:, :], ALU.mult).then_inc(dve_stat, 1)
                elif step == 3:
                    vec.tensor_tensor(vt[:, 0, :], vt[:, 0, :], vt[:, 1, :], ALU.mult).then_inc(dve_stat, 1)
                elif step == 4:
                    vec.scalar_tensor_tensor(out=s_t[:, :], in0=vt[:, 0, :], scalar=1.5, in1=s_t[:, :], op0=ALU.add,
                                             op1=ALU.mult).then_inc(dve_stat, 1)
                else:
                    vec.tensor_tensor(b_t[:, :], ps[:, 64:64 + G], s_t[:, :], ALU.mult).then_inc(st_done, 1)

            def x_low(n, i):
                t, c = divmod(i, Q)
                r0, nr = TILES[t]
                vec.wait_ge(xs_hi, n * UNITS + i + 1)
                vec.scalar_tensor_tensor(out=xs[:, i % XS_RING, 1, 0:nr * W], in0=xb[:, c, r0 * W:(r0 + nr) * W],
                                         scalar=negm[:, c:c + 1], in1=f32(xs[:, i % XS_RING, 0, 0:nr * W]),
                                         op0=ALU.add, op1=ALU.subtract).then_inc(xs_lo, 1)

            def f_low(n, t):
                r0, nr = TILES[t]
                vec.wait_ge(f_hi, n * NT + t + 1)
                vec.scalar_tensor_tensor(out=fl[:, r0 + 1:r0 + 1 + nr, 1:W + 1],
                                         in0=pac[t % 2][:, 0:nr * W].rearrange("p (r w) -> p r w", w=W), scalar=0.0,
                                         in1=f32(fh[:, r0 + 1:r0 + 1 + nr, 1:W + 1]), op0=ALU.max,
                                         op1=ALU.subtract).then_inc(f_lo, 1)

            def y_low(n, t):
                nr = TILES[t][1]
                vec.wait_ge(y_hi, n * NT + t + 1)
                vec.scalar_tensor_tensor(out=xs[:, t % 2, 1, 0:nr * W], in0=pb[t % 2][:, 0:nr * W], scalar=badc[:, 0:1],
                                         in1=f32(xs[:, t % 2, 0, 0:nr * W]), op0=ALU.add,
                                         op1=ALU.subtract).then_inc(y_lo, 1)

            def residual(n, t, c):
                if t == 0 and c == 0:
                    reached(vec, x1_out, n * 80)
                vec.wait_ge(c_mm, n * UNITS + t * Q + c + 1)
                acc = pac[(t * Q + c) % C_BANKS]
                r0 = TILES[t][0]
                for j, (r, m) in enumerate(PARTS[t]):
                    k, b = r % OR_, r // OR_
                    vec.scalar_tensor_tensor(
                        out=x1b[:, c, k:k + m, b, :], in0=acc[:, (r - r0) * W:(r - r0 + m) * W].rearrange("p (r w) -> p r w", w=W),
                        scalar=bfc[:, c:c + 1], in1=xb[:, c, r * W:(r + m) * W].rearrange("p (r w) -> p r w", w=W),
                        op0=ALU.add, op1=ALU.add,
                        accum_out=sums[:, c, PART_SUM[t] + j:PART_SUM[t] + j + 1]).then_inc(x1_done, 1)

            def output(n, g):
                vec.wait_ge(d_mm, n * G + g + 1)
                dst = t_slot(g // GQ)[0:M6, g % GQ]
                vec.scalar_tensor_tensor(out=dst, in0=pd[g % 2][0:M6, 0:BW].rearrange("p (b w) -> p b w", w=W),
                                         scalar=kout[0:M6, 2:3], in1=dst, op0=ALU.mult, op1=ALU.add).then_inc(out_done, 1)

            def step(n, d=True, more=True):
                for t in range(NT):
                    for i in range(t * Q, (t + 1) * Q):
                        if i >= len(AT_X_LOW) or not d:
                            x_low(n, i)
                        if d and 0 <= i - AT_SCALES < SCALE_STEPS:
                            x1_scales(n - 1, i - AT_SCALES)
                    if t:
                        f_low(n, t - 1)
                f_low(n, NT - 1)
                dyn_steps = [dyn_inputs, dyn_maxima, dyn_maxima, dyn_global, dyn_global]
                h = 0
                for g in range(D_FIRST):
                    if d:
                        output(n - 1, g)
                    if dyn_steps:
                        dyn_steps.pop(0)(n, DYN_HALVES[g % 2])
                    if g == DYN_LOW_AT:
                        dyn_low(n)
                    if more and g in PREP_AT:
                        prep_half(n + 1, h)
                        h += 1
                for _ in range(PREP_IN_B[0] if more else 0):
                    prep_half(n + 1, h)
                    h += 1
                y_low(n, 0)
                for _ in range(PREP_IN_B[1] if more else 0):
                    prep_half(n + 1, h)
                    h += 1
                for t in range(1, NT):
                    for c in range(Q):
                        if c == Q - 1:
                            y_low(n, t)
                        residual(n, t - 1, c)
                        if more and c < Q - 1:
                            prep_half(n + 1, h)
                            h += 1
                for g in range(D_FIRST, G):
                    for c in LATE.get(g, ()):
                        residual(n, NT - 1, c)
                    if d:
                        output(n - 1, g)
                    if g == AT_X1_SUMS:
                        x1_means(n)
                    if g == AT_X1_MEANS:
                        x1_group_means(n)
                    if g == AT_X1_VARIANCES:
                        x1_variances(n)
                    if more:
                        if g == AT_MEANS:
                            prep_means(n + 1)
                        if g == AT_VARIANCES:
                            prep_variances(n + 1)
                        if AT_SCALED <= g < AT_SCALED + 3:
                            prep_scaled(n + 1, g - AT_SCALED)
                        if g in AT_X_LOW:
                            x_low(n + 1, AT_X_LOW.index(g))

            constants()
            vec.wait_ge(pool_const, 6)
            for h in range(2 * PIECES):
                prep_half(0, h, first=True)
            prep_means(0)
            prep_variances(0)
            for i in range(3):
                prep_scaled(0, i)
            images(vec, step)
            for i in range(SCALE_STEPS):
                x1_scales(N - 1, i)
            for g in range(G):
                output(N - 1, g)

        @block.tensor
        def _(pe):
            def three(acc, high_w, low_w, high_x, low_x, start, stop):
                pe.matmul(acc, high_w, high_x, start=start, stop=False)
                pe.matmul(acc, high_w, low_x, start=False, stop=False)
                return pe.matmul(acc, low_w, high_x, start=False, stop=stop)

            def a_tile(n, t):
                nr = TILES[t][1]
                if t >= 2:
                    pe.wait_ge(f_lo, n * NT + t - 1)
                acc = pac[t % 2][:, 0:nr * W]
                pe.matmul(acc.rearrange("p (r w) -> p r w", w=W), bmat[:, :], onesr[:, :].unsqueeze(1).to_broadcast([P, nr, W]),
                          start=True, stop=False)
                for c in range(Q):
                    i = t * Q + c
                    pe.wait_ge(xs_lo, n * UNITS + i + 1)
                    three(acc, wch[:, c, :], wcl[:, c, :], xs[:, i % XS_RING, 0, 0:nr * W], xs[:, i % XS_RING, 1, 0:nr * W],
                          False, c == Q - 1).then_inc(a_mm, 1)

            def c_unit(n, t, c):
                nr = TILES[t][1]
                if c == 0:
                    pe.wait_ge(y_lo, n * NT + t + 1)
                i = t * Q + c
                if i >= C_BANKS:
                    j = i - C_BANKS
                    pe.wait_ge(x1_done, n * X1_OPS + x1_count(j // Q, j % Q))
                three(pac[i % C_BANKS][:, 0:nr * W], wfh[:, c * P:(c + 1) * P], wfl[:, c * P:(c + 1) * P],
                      xs[:, t % 2, 0, 0:nr * W], xs[:, t % 2, 1, 0:nr * W], True, True).then_inc(c_mm, 1)

            def b_tile(n, t):
                r0, nr = TILES[t]
                pe.wait_ge(f_lo, n * NT + min(t + 2, NT))
                reached(pe, y_lo, n * NT + t - 1 if t >= 2 else n * NT)
                acc = pb[t % 2][:, 0:nr * W].rearrange("p (r w) -> p r w", w=W)
                for k in range(TAPS):
                    dy, dx = divmod(k, 3)
                    ins = three(acc, dynh[:, k, :], dynl[:, k, :], fh[:, r0 + dy:r0 + dy + nr, dx:dx + W],
                                fl[:, r0 + dy:r0 + dy + nr, dx:dx + W], k == 0, k == TAPS - 1)
                    if k == TAPS - 1:
                        ins.then_inc(b_mm, 1)
                    if t and k in C_AFTER:
                        c_unit(n, t - 1, C_AFTER.index(k))

            def d_group(n, g):
                pe.wait_ge(hl_lo, n * G + g + 1)
                reached(pe, out_done, n * G + g - 1)
                acc = pd[g % 2][0:M6, 0:BW].rearrange("p (b w) -> p b w", w=W)
                s = g % HL_RING
                for dx in range(3):
                    ins = three(acc, k_h[:, g, dx, :], k_l[:, g, dx, :], hl[:, s, 0, :, dx:dx + W], hl[:, s, 1, :, dx:dx + W],
                                dx == 0, dx == 2)
                ins.then_inc(d_mm, 1)

            def group_mean(n):
                pe.wait_ge(stat_ready, 3 * n + 1)
                pe.matmul(ps[:, 0:Q], ind_m, mv[:, :, 0], start=True, stop=True).then_inc(stat_mm, 1)

            def group_variance(n):
                pe.wait_ge(stat_ready, 3 * n + 2)
                pe.matmul(ps[:, 8:8 + Q], ind_m, va[:, 2, :], start=True, stop=True).then_inc(stat_mm, 1)

            def kernel_inputs(n):
                pe.wait_ge(stat_ready, 3 * n + 3)
                pe.wait_ge(cent_done, n + 1)
                for c in range(Q):
                    ins = pe.matmul(ps[:, 16:16 + TAPS + 1], wcs[:, c, :], cent[:, c, :], start=c == 0, stop=c == Q - 1)
                ins.then_inc(stat_mm, 1)

            def x1_group_means(n):
                pe.wait_ge(nmean_done, n + 1)
                pe.matmul(ps[:, 32:32 + Q], ind_m, nmean[:, :], start=True, stop=True).then_inc(stat_mm2, 1)

            def x1_spread(n):
                pe.wait_ge(stat_ready2, n + 1)
                pe.matmul(ps[:, 64:64 + 2 * G], ones[:, :], spread[:, :, :, :].rearrange("p a q j -> p (a q j)"),
                          start=True, stop=True).then_inc(stat_mm2, 1)

            def step(n, d=True, more=True):
                pe.wait_ge(wc_done, n + 1)
                reached(pe, x1_done, n * X1_OPS)
                for t in range(NT):
                    a_tile(n, t)
                kernel_inputs(n)
                if d:
                    for g in range(D_FIRST):
                        d_group(n - 1, g)
                pe.wait_ge(dyn_done, n + 1)
                for t in range(NT):
                    b_tile(n, t)
                for g in range(D_FIRST, G):
                    for c in LATE.get(g, ()):
                        c_unit(n, NT - 1, c)
                    if d:
                        d_group(n - 1, g)
                    if g == AT_X1_MEANS:
                        x1_group_means(n)
                    if g == AT_SUMS[0] and more:
                        group_mean(n + 1)
                    if g == AT_SUMS[1] and more:
                        group_variance(n + 1)
                    if g == G - 1:
                        x1_spread(n)

            ind_m = ind[:, :, :].rearrange("p j c -> p (j c)")
            pe.wait_ge(pool_const, 6)
            pe.wait_ge(vec_const, 3)
            group_mean(0)
            group_variance(0)
            images(pe, step)
            for g in range(G):
                d_group(N - 1, g)


INPUTS = ["x", "wct", "bc", "wkk", "bkk", "wck", "bck", "b_ad", "wft", "bf", "kt"]


def kernel(x, L0_conv_Wc, L0_conv_bc, L0_conv_Wkk, L0_conv_bkk, L0_conv_Wck, L0_conv_bck, L0_conv_b_ad, L0_conv_Wf,
           L0_conv_bf, L1_conv_kernels):
    import numpy as np
    from concourse import bacc
    from concourse.bass_utils import run_bass_kernel_spmd

    laid_out = {
        "x": np.asarray(x),
        "wct": np.asarray(L0_conv_Wc).reshape(CM, Q, P).transpose(2, 1, 0),
        "bc": np.asarray(L0_conv_bc),
        "wkk": np.asarray(L0_conv_Wkk),
        "bkk": np.asarray(L0_conv_bkk),
        "wck": np.asarray(L0_conv_Wck).T,
        "bck": np.asarray(L0_conv_bck),
        "b_ad": np.asarray(L0_conv_b_ad),
        "wft": np.asarray(L0_conv_Wf).T,
        "bf": np.asarray(L0_conv_bf).reshape(Q, P).T,
        "kt": np.asarray(L1_conv_kernels).reshape(G, GC, GC, 3, 3).transpose(2, 0, 4, 3, 1)[:, :, :, ::-1, :].reshape(GC, G * 3, 3 * GC),
    }
    nc = bacc.Bacc("TRN2", target_bir_lowering=False, num_devices=1, dynamic_dma_scratch_size=1024)
    arrays, aps = {}, {}
    for name in INPUTS:
        a = np.ascontiguousarray(laid_out[name])
        arrays[name] = a
        aps[name] = nc.dram_tensor(name, a.shape, mybir.dt.from_np(a.dtype), kind="ExternalInput").ap()
    out = nc.dram_tensor("out", (N, Q, M6, GQ * BW), F32, kind="ExternalOutput").ap()
    build(nc, *[aps[name] for name in INPUTS], out)
    r = run_bass_kernel_spmd(nc, [arrays], core_ids=[0])
    got = r.results[0]["out"].reshape(N, Q, OR_, GC, GQ, NB, W)
    return np.ascontiguousarray(got.transpose(0, 1, 4, 3, 5, 2, 6)).reshape(N, C, H, W)
```
